# Optimizing a Trainium2 kernel written in Bass

```python
import numpy as np
import jax
import jax.numpy as jnp

def _softmax(x, axis=-1):
    return jax.nn.softmax(x, axis=axis)

def _gelu(x):
    return jax.nn.gelu(x, approximate=True)

def _silu(x):
    return jax.nn.silu(x)

def _sigmoid(x):
    return jax.nn.sigmoid(x)

def _layernorm(x, axis=-1, eps=1e-05):
    m = jnp.mean(x, axis=axis, keepdims=True)
    v = jnp.var(x, axis=axis, keepdims=True)
    return (x - m) / jnp.sqrt(v + eps)

def _scatter_add(tgt, idx, src, axis=0):
    return tgt.at[idx].add(src)

def _segment_sum(src, seg, n):
    return jax.ops.segment_sum(src, seg, n)
kernel_name = 'mk_gnn_preln_d2_gnn_r64_57b8d2'

def setup_inputs(seed: int=0):
    np.random.seed(seed)
    _w = jnp.asarray

    def _rec_inputs():
        import jax
        import jax.numpy as jnp
        _gk = jax.random.key(seed)
        x = -0.000202 + 1 * jax.random.normal(jax.random.fold_in(_gk, 1), (100000, 64), jnp.float32)
        src = jax.random.randint(jax.random.fold_in(_gk, 2), (25000,), 0, 100000, jnp.int32)
        dst = jax.random.randint(jax.random.fold_in(_gk, 3), (25000,), 0, 100000, jnp.int32)
        _o = jnp.argsort(dst, stable=True)
        src = src[_o]
        dst = dst[_o]
        edge_attr_32 = -5.3897e-05 + 0.999841 * jax.random.normal(jax.random.fold_in(_gk, 12), (25000, 32), jnp.float32)
        return (x, src, dst, edge_attr_32)
    x, src, dst, edge_attr_32 = _rec_inputs()

    def _L0_gnn_setup():
        import jax, jax.numpy as jnp
        import numpy as np
        N_NODES = 100000
        N_EDGES = 25000
        D_IN = 64
        D_OUT = 64
        BN_EPS = 1e-05
        key = jax.random.key(seed)
        ks = jax.random.split(key, 8)
        feat = jax.random.normal(ks[0], (N_NODES, D_IN), dtype=jnp.float32)
        src = jax.random.randint(ks[1], (N_EDGES,), 0, N_NODES, dtype=jnp.int64 if jax.config.jax_enable_x64 else jnp.int32)
        dst = jax.random.randint(ks[2], (N_EDGES,), 0, N_NODES, dtype=jnp.int64 if jax.config.jax_enable_x64 else jnp.int32)
        W_conv = jax.random.normal(ks[3], (D_IN, D_OUT), dtype=jnp.float32) * (1.0 / np.sqrt(D_IN))
        b_conv = jnp.zeros((D_OUT,), dtype=jnp.float32)
        W_res = jax.random.normal(ks[4], (D_IN, D_OUT), dtype=jnp.float32) * (1.0 / np.sqrt(D_IN))
        b_res = jnp.zeros((D_OUT,), dtype=jnp.float32)
        gamma = jnp.ones((D_OUT,), dtype=jnp.float32)
        beta = jnp.zeros((D_OUT,), dtype=jnp.float32)
        return {'feat': feat, 'W_conv': W_conv, 'b_conv': b_conv, 'W_res': W_res, 'b_res': b_res, 'gamma': gamma, 'beta': beta, 'src': src, 'dst': dst}
    _L0_gnn_all = _L0_gnn_setup()
    _L0_gnn_in = {k: v for k, v in _L0_gnn_all.items() if k in ('W_conv', 'b_conv', 'W_res', 'b_res', 'gamma', 'beta')}
    del _L0_gnn_all

    def _L1_gnn_setup():
        import jax, jax.numpy as jnp
        import numpy as np
        N_NODES = 50000
        N_EDGES = 12500
        D_NODE = 64
        D_EDGE = 32
        H_MSG = (2 * D_NODE + D_EDGE) // 2
        H_CMB = 3 * D_NODE // 2

        def _gelu(x):
            return jax.nn.gelu(x, approximate=False)
        key = jax.random.key(seed)
        ks = jax.random.split(key, 11)

        def lin(k, fan_in, fan_out):
            bound = 1.0 / np.sqrt(fan_in)
            k1, k2 = jax.random.split(k)
            W = jax.random.uniform(k1, (fan_in, fan_out), jnp.float32, -bound, bound)
            b = jax.random.uniform(k2, (fan_out,), jnp.float32, -bound, bound)
            return (W, b)
        node_vectors = jax.random.normal(ks[0], (N_NODES, D_NODE), jnp.float32)
        edge_vectors = jax.random.normal(ks[1], (N_EDGES, D_EDGE), jnp.float32)
        edge_indices = jax.random.randint(ks[2], (N_EDGES, 2), 0, N_NODES, jnp.int64 if jax.config.jax_enable_x64 else jnp.int32)
        W_m1, b_m1 = lin(ks[3], 2 * D_NODE + D_EDGE, H_MSG)
        W_m2, b_m2 = lin(ks[4], H_MSG, D_NODE)
        W_c1, b_c1 = lin(ks[5], 2 * D_NODE, H_CMB)
        W_c2, b_c2 = lin(ks[6], H_CMB, D_NODE)
        return {'node_vectors': node_vectors, 'edge_vectors': edge_vectors, 'edge_indices': edge_indices, 'W_m1': W_m1, 'b_m1': b_m1, 'W_m2': W_m2, 'b_m2': b_m2, 'W_c1': W_c1, 'b_c1': b_c1, 'W_c2': W_c2, 'b_c2': b_c2}
    _L1_gnn_all = _L1_gnn_setup()
    _L1_gnn_in = {k: v for k, v in _L1_gnn_all.items() if k in ('W_m1', 'b_m1', 'W_m2', 'b_m2', 'W_c1', 'b_c1', 'W_c2', 'b_c2')}
    del _L1_gnn_all
    return {'x': x, 'src': src, 'dst': dst, 'edge_attr_32': edge_attr_32, 'L0_gnn_W_conv': _L0_gnn_in['W_conv'], 'L0_gnn_b_conv': _L0_gnn_in['b_conv'], 'L0_gnn_W_res': _L0_gnn_in['W_res'], 'L0_gnn_b_res': _L0_gnn_in['b_res'], 'L0_gnn_gamma': _L0_gnn_in['gamma'], 'L0_gnn_beta': _L0_gnn_in['beta'], 'L1_gnn_W_m1': _L1_gnn_in['W_m1'], 'L1_gnn_b_m1': _L1_gnn_in['b_m1'], 'L1_gnn_W_m2': _L1_gnn_in['W_m2'], 'L1_gnn_b_m2': _L1_gnn_in['b_m2'], 'L1_gnn_W_c1': _L1_gnn_in['W_c1'], 'L1_gnn_b_c1': _L1_gnn_in['b_c1'], 'L1_gnn_W_c2': _L1_gnn_in['W_c2'], 'L1_gnn_b_c2': _L1_gnn_in['b_c2']}

def reference(x, src, dst, edge_attr_32, L0_gnn_W_conv, L0_gnn_b_conv, L0_gnn_W_res, L0_gnn_b_res, L0_gnn_gamma, L0_gnn_beta, L1_gnn_W_m1, L1_gnn_b_m1, L1_gnn_W_m2, L1_gnn_b_m2, L1_gnn_W_c1, L1_gnn_b_c1, L1_gnn_W_c2, L1_gnn_b_c2):
    import jax
    import jax.numpy as jnp

    def _L0_gnn_ref(feat, W_conv, b_conv, W_res, b_res, gamma, beta, src, dst):
        import jax, jax.numpy as jnp
        import numpy as np
        N_NODES = 100000
        N_EDGES = 25000
        D_IN = 64
        D_OUT = 64
        BN_EPS = 1e-05
        score = jnp.sum(feat[src] * feat[dst], axis=-1)
        smax = jax.ops.segment_max(score, dst, num_segments=N_NODES)
        ez = jnp.exp(score - smax[dst])
        denom = jax.ops.segment_sum(ez, dst, num_segments=N_NODES)
        a = ez / denom[dst]
        ft = feat @ W_conv + b_conv
        msg = ft[src] * a[:, None]
        agg = jax.ops.segment_sum(msg, dst, num_segments=N_NODES)
        out = agg + jax.nn.relu(feat @ W_res + b_res)
        mean = jnp.mean(out, axis=0)
        var = jnp.mean((out - mean) ** 2, axis=0)
        out = (out - mean) * jax.lax.rsqrt(var + BN_EPS) * gamma + beta
        return out

    def _L1_gnn_ref(node_vectors, edge_vectors, edge_indices, W_m1, b_m1, W_m2, b_m2, W_c1, b_c1, W_c2, b_c2):
        import jax, jax.numpy as jnp
        import numpy as np
        N_NODES = 50000
        N_EDGES = 12500
        D_NODE = 64
        D_EDGE = 32
        H_MSG = (2 * D_NODE + D_EDGE) // 2
        H_CMB = 3 * D_NODE // 2

        def _gelu(x):
            return jax.nn.gelu(x, approximate=False)
        node_i = node_vectors[edge_indices[:, 0]]
        node_j = node_vectors[edge_indices[:, 1]]
        msg_input = jnp.concatenate([node_i, node_j, edge_vectors], axis=1)
        h = _gelu(msg_input @ W_m1 + b_m1)
        messages = _gelu(h @ W_m2 + b_m2)
        boxes = jax.ops.segment_sum(messages, edge_indices[:, 1], num_segments=node_vectors.shape[0])
        pairs = jnp.concatenate([node_vectors, boxes], axis=1)
        c = _gelu(pairs @ W_c1 + b_c1)
        combined = _gelu(c @ W_c2 + b_c2)
        return node_vectors + combined
    edge_index_t = jnp.stack([src, dst], axis=1)
    h = jnp.maximum(_layernorm(x, axis=-1), 0.0)
    x = x + _L0_gnn_ref(h, L0_gnn_W_conv, L0_gnn_b_conv, L0_gnn_W_res, L0_gnn_b_res, L0_gnn_gamma, L0_gnn_beta, src, dst)
    h = jnp.maximum(_layernorm(x, axis=-1), 0.0)
    x = x + _L1_gnn_ref(h, edge_attr_32, edge_index_t, L1_gnn_W_m1, L1_gnn_b_m1, L1_gnn_W_m2, L1_gnn_b_m2, L1_gnn_W_c1, L1_gnn_b_c1, L1_gnn_W_c2, L1_gnn_b_c2)
    return x

_drawn_inputs = setup_inputs


def setup_inputs(seed=0):
    import zlib

    import numpy as np

    out = dict(_drawn_inputs(seed))
    spreads = {'L0_gnn_b_conv': (0.0, 0.1),
     'L0_gnn_b_res': (0.0, 0.1),
     'L0_gnn_gamma': (1.0, 0.2),
     'L0_gnn_beta': (0.0, 0.1)}
    factors = {'edge_attr_32': 8.0,
     'L1_gnn_W_m1': 8.0,
     'L1_gnn_b_m1': 24.235,
     'L1_gnn_W_m2': 8.0,
     'L1_gnn_b_m2': 58.358,
     'L1_gnn_b_c1': 8.0,
     'L1_gnn_b_c2': 3.912}
    for name, (base, spread) in spreads.items():
        noise = np.random.default_rng([zlib.crc32(name.encode()), seed]).standard_normal(out[name].shape)
        drawn = base * np.exp(spread * noise) if base else spread * noise
        out[name] = jnp.asarray(drawn.astype(out[name].dtype))
    for name, factor in factors.items():
        out[name] = (out[name] * factor).astype(out[name].dtype)
    return out
```

```python
from contextlib import ExitStack

import concourse.bass as bass
from concourse import mybir

F32 = mybir.dt.float32
BF16 = mybir.dt.bfloat16
I32 = mybir.dt.int32
ALU = mybir.AluOpType
ACT = mybir.ActivationFunctionType
AX = mybir.AxisListType.X

P = 128
D = 64
DE = 32
EP = 125
EJ = 4
EG = EP * EJ
R = 16
RD = R * D
PAIRS = R // 2
STEP = P * R
LN_EPS = 1e-5
BN_EPS = 1e-5
SHIFT = 32.0
BEYOND = 1048576
MAGIC = float(0x5F3759DF)
NEWTON = 10


class Stage:

    def __init__(self, sem, incs=1):
        self.sem, self.incs = sem, incs

    def done(self, eng, step):
        if isinstance(step, int) and step < 0:
            return
        eng.wait_ge(self.sem, step * self.incs + self.incs)

    def part(self, eng, step, k):
        eng.wait_ge(self.sem, step * self.incs + k)


class Slots:

    def __init__(self, sems, incs=16):
        self.sems, self.incs = sems, incs

    def done(self, eng, half, q):
        if isinstance(half, int) and half < 0:
            return
        eng.wait_ge(self.sems[q], half * self.incs + self.incs)


def program(nc, t, out):
    x, src, dst, ea = t["x"], t["src"], t["dst"], t["edge_attr_32"]
    N = x.shape[0]
    E = src.shape[0]
    G = E // EG
    NS = N // STEP
    PT = (N - NS * STEP) // R
    BODY = NS // 4
    GB = G // 2
    LOOPED = GB - 4
    assert G * EG == E and NS % 4 == 0 and PT * R + NS * STEP == N and PT <= P and G % 2 == 0
    assert N < 1 << 20 and 2 * BODY < G
    H1 = t["L1_gnn_W_m1"].shape[1]
    H2 = t["L1_gnn_W_c1"].shape[1]

    with ExitStack() as ctx:
        def sb(name, shape, dt=F32):
            return ctx.enter_context(nc.sbuf_tensor(name, shape, dt))

        def pb(name):
            return ctx.enter_context(nc.psum_tensor(name, [P, 512], F32))

        def sem(name):
            return ctx.enter_context(nc.semaphore(name))

        def stage(name, incs=1):
            return Stage(sem(name), incs)

        def slots(name, incs=16):
            return Slots([sem(name + "0"), sem(name + "1")], incs)

        table = nc.dram_tensor("layer0_rows", (N, D), F32).ap()
        edge_rows = nc.dram_tensor("edge_rows", (G, EP, 2 * EJ * D), F32).ap()
        dst_pad = nc.dram_tensor("dst_pad", (E + 2,), I32).ap()
        same_row = nc.dram_tensor("same_row", (E,), F32).ap()
        put_row = nc.dram_tensor("put_row", (E,), I32).ap()

        ident = sb("ident", [P, P])
        ones = sb("ones", [P, P])
        ones16 = sb("ones16", [D + 1, P], BF16)
        shift = sb("shift", [P, 1])
        wres2 = sb("wres2", [P, P])
        wconv = sb("wconv", [D + 1, D + 1])
        bias_in = sb("bias_in", [D + 1, 2, D])
        bias_rest = sb("bias_rest", [D + 1, 2, 2, D])
        bias_part = sb("bias_part", [D + 1, 3, 2, D], BF16)
        bias16 = sb("bias16", [D + 1, 2, 8, D], BF16)
        wc1_node = sb("wc1_node", [P, H2])
        wc1 = sb("wc1", [P, H2])
        wc2 = sb("wc2", [H2, D])
        wm1_dst = sb("wm1_dst", [D, H1])
        wm1_rest = sb("wm1_rest", [D + DE, H1])
        wm2 = sb("wm2", [H1, P])
        bm1 = sb("bm1", [H1, 1])
        bm2 = sb("bm2", [P, 1])
        bc1 = sb("bc1", [H2, 1])
        bn_in = sb("bn_in", [P, 2, D])
        bn = sb("bn", [P, 2, D])

        dst_idx = sb("dst_idx", [EP, G * EJ], I32)
        next_idx = sb("next_idx", [EP, G * EJ], I32)
        put_idx = sb("put_idx", [EP, G * EJ], I32)
        get_idx = [sb(f"get_idx{q}", [EP, 2 * EJ], I32) for q in range(2)]
        put_now = [sb(f"put_now{i}", [EP, EJ], I32) for i in range(4)]
        put_rows = [sb(f"put_rows{i}", [EP, EJ * D]) for i in range(4)]
        last = sb("last", [EP, G * EJ])
        flat = sb("flat", [EP, 2, E // EP], I32)
        same_flat = sb("same_flat", [EP, E // EP])
        end_mark = sb("end_mark", [1, 2], I32)

        xin = [sb(f"xin{q}", [P, RD]) for q in range(2)]
        rin = [sb(f"rin{q}", [P, RD]) for q in range(2)]
        xc = [sb(f"xc{q}", [P, RD]) for q in range(2)]
        x2 = [sb(f"x2_{q}", [P, RD]) for q in range(2)]
        sq = sb("sq", [P, RD])
        hT = sb("hT", [P, RD])
        res = [sb(f"res{q}", [P, RD]) for q in range(2)]
        cT = sb("cT", [H2, 2, 512])
        stat = sb("stat", [P, 6, R])

        eg = [sb(f"eg{q}", [EP, 2 * EJ * D]) for q in range(2)]
        er = [sb(f"er{q}", [EP, 2 * EJ * D]) for q in range(2)]
        ec = sb("ec", [EP, 2 * EJ * D])
        ex = sb("ex", [EP, 2 * EJ * D])
        esq = sb("esq", [EP, 2 * EJ * D])
        estat = sb("estat", [EP, 6, 2 * EJ])
        prod = sb("prod", [EP, EJ * D])
        score = sb("score", [EP, EJ])
        weighted = sb("weighted", [EP, EJ, D + 1])
        same = [sb(f"same{q}", [P, EG]) for q in range(2)]
        sums = [sb(f"sums{q}", [D + 1, EG]) for q in range(2)]
        hdT = sb("hdT", [D, EG])
        rdst = sb("rdst", [EP, EJ * D])
        inv = sb("inv", [EP, EJ])
        diff = sb("diff", [EP, EJ, 2 * D])
        twice = sb("twice", [EP, EJ * D])
        dst_rows = sb("dst_rows", [EP, G * EJ * D])
        hsrc = [sb(f"hsrc{q}", [EP, EJ, D + DE]) for q in range(2)]
        hdst = sb("hdst", [EP, EJ * D])
        restT = sb("restT", [D + DE, EG])
        m1T = sb("m1T", [H1, EG])
        m2T = sb("m2T", [P, EG])
        pairT = [sb(f"pairT{q}", [P, EG]) for q in range(2)]
        ecT = sb("ecT", [H2, EG])
        eadd = sb("eadd", [EP, EJ * D])

        bnz = sb("bnz", [P, 2, 2, D])
        bncol = sb("bncol", [P, 4])
        bndiag = sb("bndiag", [P, P])
        bnw = sb("bnw", [P, 8, D])

        B = [pb(f"bank{i}") for i in range(8)]
        bank_t, bank_r, bank_sum = B[0:2], B[2:4], B[4]
        bank_w, bank_d, bank_a = B[5], B[6], B[7]
        bank_h, bank_c, bank_o = B[0], B[1:3], B[3]
        bank_e1, bank_e2, bank_m, bank_q = B[4], B[5], B[6], B[7]

        s_w = sem("weights_loaded")
        s_puts = sem("put_row_stored")
        S_ix = slots("get_idx_loaded", 32)
        S_px = [sem(f"put_idx_loaded{i}") for i in range(4)]
        L_ix = slots("get_idx_reloaded", 32)
        L_px = [sem(f"final_put_idx_loaded{i}") for i in range(4)]
        s_dst = sem("dst_loaded")
        s_pad = sem("dst_padded")
        s_flat = sem("dst_windows_loaded")
        s_sameput = sem("same_row_stored")
        s_c = sem("pool_constants")
        s_v = sem("vector_setup")
        s_zero = sem("sums_bank_cleared")
        S_x = slots("x_loaded")
        S_center = stage("centered", 2)
        S_sq = stage("squared")
        S_h = stage("h_ready", NEWTON + 3)
        S_t = stage("h_transposed", 2)
        S_ht = stage("hT_copied", 2)
        S_r = stage("r_product", 2)
        S_relu = stage("r_ready", 2)
        S_gram = stage("r_summed")
        S_st = slots("r_stored")
        S_eg = slots("edge_x_gathered", 16 * 2 * EJ)
        S_esv = slots("edge_x_stashed")
        S_same = slots("same_loaded")
        S_ea = stage("edge_centered", 2)
        S_esq = stage("edge_squared")
        S_eb = stage("edge_scored", NEWTON + 5)
        S_exp = stage("edge_exp")
        S_ew = stage("edge_weighted")
        S_et = stage("edge_transposed")
        S_hd = stage("hdT_copied")
        S_scan = stage("segment_summed")
        S_agg = stage("edge_products", 2)
        S_rd = stage("r_of_dst")
        S_ee = stage("dst_row_ready", 5)
        S_es = stage("edge_stats_added")
        s_put = sem("layer0_rows_scattered")
        s_bnp = sem("bn_summed")
        s_bnd = sem("bn_vector")
        L_x = slots("rows_loaded", 32)
        L_f = stage("x2_centered", 5)
        L_sq = stage("x2_squared")
        L_g = stage("h2_ready", NEWTON + 4)
        L_t = stage("h2_transposed", 2)
        L_ht = stage("h2T_copied", 2)
        L_c = stage("c_product", 2)
        L_cg = stage("c_gelu", 2)
        L_o = stage("out_product", 2)
        L_og = stage("out_gelu", 2)
        L_y = stage("final_row_ready")
        L_st = slots("final_rows_stored")
        M_ld = slots("edge_stash_loaded", 32)
        M_er = slots("layer0_rows_gathered", 16 * 2 * EJ)
        M_same = slots("same_reloaded")
        M_a = stage("edge_x2_centered", 5)
        M_sq = stage("edge_x2_squared")
        M_b = stage("edge_h2_ready", NEWTON + 5)
        M_t = stage("edge_h2_transposed", 2)
        M_tc = stage("edge_h2T_copied", 2)
        M_m1 = stage("message1_product")
        M_g1 = stage("message1_gelu")
        M_m2 = stage("message2_product")
        M_g2 = stage("message2_gelu")
        M_scan = stage("messages_summed")
        M_c = stage("edge_c_product")
        M_cg = stage("edge_c_gelu")
        M_o = stage("edge_out_product")
        M_og = stage("edge_out_gelu")
        M_y = stage("dst_final_ready")
        s_fput = sem("final_rows_scattered")

        main = NS * STEP

        def dense_rows(a, s, p):
            if p == P:
                v = a[0:main, :].rearrange("(s p r) d -> s p (r d)", p=P, r=R)
                return v[s, :, :] if isinstance(s, int) else v[bass.ds(s, 1), :, :].rearrange("a p n -> (a p) n")
            return a[main:N, :].rearrange("(p r) d -> p (r d)", r=R)

        def one(a, g):
            if isinstance(g, int):
                return a[g]
            v = a[bass.ds(g, 1)]
            return v.rearrange("a p n -> (a p) n") if len(v.shape) == 3 else v.rearrange("a n -> (a n)")

        def rows(a):
            return a.rearrange("p (r d) -> p r d", d=D)

        def per_row(a, n=D):
            return a.unsqueeze(2).broadcast_to([a.shape[0], a.shape[1], n])

        def cols(a, w):
            return a.unsqueeze(1).broadcast_to([a.shape[0], w, a.shape[1]])

        def group_cols(t2, g, w=EJ * D):
            return t2[:, bass.ds(g * w, w)] if not isinstance(g, int) else t2[:, g * w:g * w + w]

        block = ctx.enter_context(nc.Block())

        @block.sync
        def _(sp):
            def load_small(dst_ap, src_ap):
                sp.dma_start(dst_ap, src_ap).then_inc(s_w, 16)

            def edge_values(a, g):
                return one(a.rearrange("(g p j) -> g p j", p=EP, j=EJ), g)

            def load_idx(g, q, done):
                done()
                sp.dma_start(get_idx[q][:, 0:EJ], edge_values(src, g)).then_inc(S_ix.sems[q], 16)
                sp.dma_start(get_idx[q][:, EJ:2 * EJ], edge_values(dst, g)).then_inc(S_ix.sems[q], 16)

            load_idx(0, 0, lambda: None)
            load_idx(1, 1, lambda: None)
            sp.dma_start(dst_idx[:, :].rearrange("p (g j) -> p g j", j=EJ),
                         dst.rearrange("(g p j) -> p g j", p=EP, j=EJ)).then_inc(s_dst, 16)

            def col(a):
                return a.rearrange("(n a) -> n a", a=1)

            def row(a):
                return a.rearrange("(a n) -> a n", a=1)

            sp.wait_ge(s_v, 1)
            load_small(wres2[0:D, 0:D], t["L0_gnn_W_res"])
            load_small(wres2[D:P, D:P], t["L0_gnn_W_res"])
            load_small(wconv[0:D, 0:D], t["L0_gnn_W_conv"])
            load_small(wconv[D:D + 1, 0:D], row(t["L0_gnn_b_conv"]))
            for p in (0, 32, 64):
                load_small(bias_in[p:p + 1, 0, :], row(t["L0_gnn_b_res"]))
                load_small(bias_in[p:p + 1, 1, :], row(t["L1_gnn_b_c2"]))
            load_small(wc1_node[0:D, :], t["L1_gnn_W_c1"][0:D, :])
            load_small(wc1_node[D:P, :], t["L1_gnn_W_c1"][0:D, :])
            load_small(wc1[:, :], t["L1_gnn_W_c1"])
            load_small(wc2[:, :], t["L1_gnn_W_c2"])
            load_small(wm1_dst[:, :], t["L1_gnn_W_m1"][D:2 * D, :])
            load_small(wm1_rest[0:D, :], t["L1_gnn_W_m1"][0:D, :])
            load_small(wm1_rest[D:D + DE, :], t["L1_gnn_W_m1"][2 * D:2 * D + DE, :])
            load_small(wm2[:, D:P], t["L1_gnn_W_m2"])
            load_small(bm1[:, :], col(t["L1_gnn_b_m1"]))
            load_small(bm2[D:P, :], col(t["L1_gnn_b_m2"]))
            load_small(bc1[:, :], col(t["L1_gnn_b_c1"]))
            load_small(bn_in[:, 0, :], row(t["L0_gnn_gamma"]).broadcast_to([P, D]))
            load_small(bn_in[:, 1, :], row(t["L0_gnn_beta"]).broadcast_to([P, D]))

            sp.dma_start(dst_pad[1:E + 1], dst).then_inc(s_pad, 16)
            sp.dma_start(dst_pad[0:1].rearrange("(a n) -> a n", a=1), end_mark[:, 0:1]).then_inc(s_pad, 16)
            sp.dma_start(dst_pad[E + 1:E + 2].rearrange("(a n) -> a n", a=1),
                         end_mark[:, 1:2]).then_inc(s_pad, 16)
            sp.wait_ge(s_pad, 48)
            for k in range(2):
                sp.dma_start(flat[:, k, :], dst_pad[k:E + k].rearrange("(p c) -> p c", p=EP))\
                  .then_inc(s_flat, 16)
            sp.dma_start(next_idx[:, :].rearrange("p (g j) -> p g j", j=EJ),
                         dst_pad[2:E + 2].rearrange("(g p j) -> p g j", p=EP, j=EJ)).then_inc(s_flat, 16)
            sp.wait_ge(s_v, 3)
            sp.dma_start(same_row.rearrange("(p c) -> p c", p=EP), same_flat[:, :]).then_inc(s_sameput, 16)
            sp.wait_ge(s_v, 4)
            sp.dma_start(put_row.rearrange("(g p j) -> p g j", p=EP, j=EJ),
                         put_idx[:, :].rearrange("p (g j) -> p g j", j=EJ)).then_inc(s_puts, 16)
            sp.wait_ge(s_sameput, 16)
            sp.wait_ge(s_puts, 16)

            def load_x(s, half, q, p=P):
                S_center.done(sp, s - 2)
                sp.dma_start(xin[q][0:p, :], dense_rows(x, s, p)).then_inc(S_x.sems[q], 16)

            def store_r(s, q, p=P):
                S_relu.done(sp, s)
                sp.dma_start(dense_rows(table, s, p), res[q][0:p, :]).then_inc(S_st.sems[q], 16)

            def load_same(g, q):
                S_scan.done(sp, g - 2)
                sp.dma_start(same[q][0:D + 1, :], one(same_row.rearrange("(g n) -> g n", n=EG), g)
                             .unsqueeze(0).broadcast_to([D + 1, EG])).then_inc(S_same.sems[q], 16)

            def stash(g, half, q, more=True):
                S_eg.done(sp, half, q)
                sp.dma_start(one(edge_rows, g), eg[q][:, :]).then_inc(S_esv.sems[q], 16)
                if more:
                    load_idx(g + 2, q, lambda: None)

            def load_put(g, i, ready, sems):
                ready.done(sp, g)
                sp.dma_start(put_now[i][:, :], edge_values(put_row, g)).then_inc(sems[i], 16)
                sp.dma_start(put_rows[i][:, :], group_cols(dst_rows, g)).then_inc(sems[i], 16)

            def puts_gone(n, scattered):
                sp.wait_ge(scattered, n * (16 * 4 * EJ) + 16 * 4 * EJ)

            def load_puts(n, ready, sems):
                for i in range(4):
                    load_put(n * 4 + i, i, ready, sems)

            def last_puts(ready, sems, scattered):
                for g in range(4 * (LOOPED - BODY) + 4, G):
                    if g % 4 == 0:
                        puts_gone(g // 4 - 1, scattered)
                    load_put(g, g % 4, ready, sems)

            def half_body(it, k, dense, more=True):
                g = it * 2 + k
                s = it * 4 + 2 * k
                if dense:
                    load_x(s + 1, it * 2 + k, 1)
                load_same(g, k)
                stash(g, it, k, more)
                if dense:
                    store_r(s - 1, 1)
                    load_x(s + 2, it * 2 + k + 1, 0)
                    store_r(s, 0)

            def first_half():
                load_x(0, 0, 0)
                load_x(1, 0, 1)
                load_same(0, 0)
                stash(0, 0, 0)
                load_x(2, 1, 0)
                store_r(0, 0)

            first_half()
            half_body(0, 1, True)
            with sp.Fori(1, BODY - 1) as it:
                half_body(it, 0, True)
                half_body(it, 1, True)
            half_body(BODY - 1, 0, True)
            it, s = BODY - 1, NS - 2
            load_x(s + 1, s // 2, 1)
            load_same(2 * it + 1, 1)
            stash(2 * it + 1, it, 1)
            store_r(s - 1, 1)
            load_x(NS, NS // 2, 0, PT)
            store_r(s, 0)
            store_r(NS - 1, 1)
            store_r(NS, 0, PT)
            load_puts(0, S_ee, S_px)
            with sp.Fori(BODY, LOOPED) as it:
                half_body(it, 0, False)
                half_body(it, 1, False)
                puts_gone(it - BODY, s_put)
                load_puts(it + (1 - BODY), S_ee, S_px)
            for it in range(LOOPED, GB):
                half_body(it, 0, False, it < GB - 1)
                half_body(it, 1, False, it < GB - 1)
            last_puts(S_ee, S_px, s_put)

            for q in range(2):
                S_st.done(sp, (NS - q) // 2, q)
                S_esv.done(sp, GB - 1, q)
            sp.wait_ge(s_put, 16 * G * EJ)

            def load_rows(s, q, p=P):
                L_f.done(sp, s - 2)
                sp.dma_start(xin[q][0:p, :], dense_rows(x, s, p)).then_inc(L_x.sems[q], 16)
                sp.dma_start(rin[q][0:p, :], dense_rows(table, s, p)).then_inc(L_x.sems[q], 16)

            def store_final(s, q, p=P):
                L_y.done(sp, s)
                sp.dma_start(dense_rows(out, s, p), x2[q][0:p, :]).then_inc(L_st.sems[q], 16)

            def load_edges(g, q):
                M_a.done(sp, g - 2)
                sp.dma_start(eg[q][:, :], one(edge_rows, g)).then_inc(M_ld.sems[q], 16)
                M_t.done(sp, g - 2)
                sp.dma_start(hsrc[q][:, :, D:D + DE],
                             one(ea.rearrange("(g p j) d -> g p (j d)", p=EP, j=EJ), g)
                             .rearrange("p (j d) -> p j d", d=DE)).then_inc(M_ld.sems[q], 16)
                M_scan.done(sp, g - 2)
                sp.dma_start(same[q][D:P, :], one(same_row.rearrange("(g n) -> g n", n=EG), g)
                             .unsqueeze(0).broadcast_to([D, EG])).then_inc(M_same.sems[q], 16)

            def load_idx2(g, half, q):
                M_er.done(sp, half - 1, q)
                sp.dma_start(get_idx[q][:, 0:EJ], edge_values(src, g)).then_inc(L_ix.sems[q], 16)
                sp.dma_start(get_idx[q][:, EJ:2 * EJ], edge_values(dst, g)).then_inc(L_ix.sems[q], 16)

            def half_body2(it, k, dense):
                g, s = it * 2 + k, it * 4 + 2 * k
                if dense:
                    load_rows(s + 1, 1)
                load_edges(g, k)
                load_idx2(g, it, k)
                if dense:
                    store_final(s - 2, 0)
                    store_final(s - 1, 1)
                    load_rows(s + 2, 0)

            load_rows(0, 0)
            load_rows(1, 1)
            load_edges(0, 0)
            load_idx2(0, 0, 0)
            load_rows(2, 0)
            half_body2(0, 1, True)
            with sp.Fori(1, BODY - 1) as it:
                half_body2(it, 0, True)
                half_body2(it, 1, True)
            half_body2(BODY - 1, 0, True)
            it, s = BODY - 1, NS - 2
            load_rows(s + 1, 1)
            load_edges(2 * it + 1, 1)
            load_idx2(2 * it + 1, it, 1)
            store_final(s - 2, 0)
            store_final(s - 1, 1)
            load_rows(NS, 0, PT)
            store_final(NS - 2, 0)
            store_final(NS - 1, 1)
            store_final(NS, 0, PT)
            load_puts(0, M_y, L_px)
            with sp.Fori(BODY, LOOPED) as it:
                half_body2(it, 0, False)
                half_body2(it, 1, False)
                puts_gone(it - BODY, s_fput)
                load_puts(it + (1 - BODY), M_y, L_px)
            for it in range(LOOPED, GB):
                half_body2(it, 0, False)
                half_body2(it, 1, False)
            last_puts(M_y, L_px, s_fput)
            for q in range(2):
                L_st.done(sp, (NS - q) // 2, q)
            sp.wait_ge(s_fput, 16 * G * EJ)

        @block.gpsimd
        def _(pool):
            nc.gpsimd.memset(ident[:, :], 0.0).then_inc(s_c, 1)
            nc.gpsimd.memset(ones[:, :], 1.0)
            nc.gpsimd.memset(ones16[:, :], 1.0)
            pool.wait_ge(s_c, 1)
            nc.gpsimd.affine_select(out=ident[:, :], in_=ident[:, :], compare_op=ALU.not_equal, fill=1.0,
                                    base=0, pattern=[[-1, P]], channel_multiplier=1).then_inc(s_c, 1)

            limit = pool.to_reg(N - 1)

            nodes = pool.to_reg(N)

            def waits_end():
                pool.reg_add(limit, nodes, -1)

            def gather(dst_ap, source, index, s):
                nc.gpsimd.indirect_dma_start(dst_ap, None, source[:, :],
                                             bass.IndirectOffsetOnAxis(ap=index, axis=0),
                                             bounds_check=limit, oob_is_err=False).then_inc(s, 16)

            def gather_x(g, half, q):
                S_ix.done(pool, half, q)
                S_ea.done(pool, g - 2)
                S_esv.done(pool, half - 1, q)
                waits_end()
                for k in range(2 * EJ):
                    gather(eg[q][:, k * D:k * D + D], x, get_idx[q][:, k:k + 1], S_eg.sems[q])

            def gather_rows(g, half, q):
                L_ix.done(pool, half, q)
                M_a.done(pool, g - 2)
                waits_end()
                for j in range(2 * EJ):
                    gather(er[q][:, j * D:j * D + D], table, get_idx[q][:, j:j + 1], M_er.sems[q])

            def scatter(n, i, target, s, loaded):
                pool.wait_ge(loaded[i], n * 32 + 32)
                waits_end()
                for j in range(EJ):
                    nc.gpsimd.indirect_dma_start(target[:, :],
                                                 bass.IndirectOffsetOnAxis(ap=put_now[i][:, j:j + 1], axis=0),
                                                 put_rows[i][:, j * D:j * D + D], None,
                                                 bounds_check=limit, oob_is_err=False).then_inc(s, 16)

            def groups(gather_g, stored, *put):
                for k in range(2):
                    gather_g(k, 0, k)
                with pool.Fori(1, BODY) as it:
                    for k in range(2):
                        gather_g(it * 2 + k, it, k)
                for q in range(2):
                    stored.done(pool, (NS - q) // 2, q)
                with pool.Fori(BODY, LOOPED) as it:
                    for k in range(2):
                        gather_g(it * 2 + k, it, k)
                    for i in range(4):
                        scatter(it - BODY, i, *put)
                for g in range(2 * LOOPED, G):
                    gather_g(g, g // 2, g % 2)
                for g in range(4 * (LOOPED - BODY), G):
                    scatter(g // 4, g % 4, *put)

            groups(gather_x, S_st, table, s_put, S_px)
            pool.wait_ge(s_put, 16 * G * EJ)
            groups(gather_rows, L_st, out, s_fput, L_px)

        @block.vector
        def _(dve):
            V = nc.vector

            def inverse_sqrt(var_sum, tmp, n_mean, eps, st, step, k0):
                v, y, a = tmp
                k = k0
                V.tensor_scalar(v, var_sum, n_mean, eps, ALU.mult, ALU.add).then_inc(st.sem, 1)
                k += 1
                st.part(dve, step, k)
                V.tensor_scalar(y.bitcast(I32), v.bitcast(I32), -0.5, MAGIC, ALU.mult, ALU.add)\
                 .then_inc(st.sem, 1)
                k += 1
                st.part(dve, step, k)
                for i in range(3):
                    V.scalar_tensor_tensor(out=a, in0=y, scalar=-0.5, in1=y, op0=ALU.mult, op1=ALU.mult)\
                     .then_inc(st.sem, 1)
                    k += 1
                    st.part(dve, step, k)
                    V.tensor_tensor(a, a, v, ALU.mult).then_inc(st.sem, 1)
                    k += 1
                    st.part(dve, step, k)
                    V.scalar_tensor_tensor(out=y, in0=a, scalar=1.5, in1=y, op0=ALU.add, op1=ALU.mult)\
                     .then_inc(st.sem, 1)
                    k += 1
                    st.part(dve, step, k)
                assert k == k0 + NEWTON + 1

            V.memset(wres2[:, :], 0.0)
            V.memset(wconv[:, :], 0.0)
            V.memset(wm2[:, :], 0.0)
            V.memset(bias_in[:, :, :], 0.0)
            V.memset(bias16[:, :, :, :], 0.0)
            V.memset(shift[:, :], -SHIFT)
            V.memset(end_mark[:, :], -1).then_inc(s_v, 1)
            dve.wait_ge(s_v, 1)
            dve.wait_ge(s_w, 16 * 23)
            V.memset(wconv[D:D + 1, D:D + 1], 1.0)
            V.tensor_copy(bias_part[:, 0, :, :], bias_in[:, :, :]).then_inc(s_v, 1)
            dve.wait_ge(s_v, 2)
            dve.wait_ge(s_flat, 48)
            V.tensor_tensor(same_flat[:, :], flat[:, 0, :], flat[:, 1, :], ALU.is_equal).then_inc(s_v, 1)
            V.tensor_tensor(last[:, :], dst_idx[:, :], next_idx[:, :], ALU.is_equal).then_inc(s_bnd, 1)
            dve.wait_ge(s_bnd, 1)
            dve.wait_ge(s_dst, 16)
            V.scalar_tensor_tensor(out=put_idx[:, :], in0=last[:, :], scalar=float(BEYOND), in1=dst_idx[:, :],
                                   op0=ALU.mult, op1=ALU.add).then_inc(s_v, 1)
            dve.wait_ge(s_v, 4)
            V.tensor_scalar(last[:, :], last[:, :], -1.0, 1.0, ALU.mult, ALU.add).then_inc(s_v, 1)
            for i in range(2):
                V.tensor_tensor(bias_rest[:, i, :, :], bias_in[:, :, :] if i == 0 else bias_rest[:, 0, :, :],
                                bias_part[:, i, :, :], ALU.subtract).then_inc(s_v, 1)
                dve.wait_ge(s_v, 6 + 2 * i)
                V.tensor_copy(bias_part[:, i + 1, :, :], bias_rest[:, i, :, :]).then_inc(s_v, 1)
                dve.wait_ge(s_v, 7 + 2 * i)
            for i in range(3):
                for b in range(2):
                    V.tensor_copy(bias16[32 * i:32 * i + 1, b, :, :],
                                  cols(bias_part[32 * i:32 * i + 1, i, b, :], 8)).then_inc(s_v, 1)
            assert D == 64

            def center(s, half, q, p=P):
                S_x.done(dve, half, q)
                if not (isinstance(s, int) and s < 2):
                    S_t.done(dve, s - 2)
                V.tensor_reduce(stat[0:p, q, :], rows(xin[q][0:p, :]), AX, ALU.add).then_inc(S_center.sem, 1)
                S_center.part(dve, s, 1)
                V.scalar_tensor_tensor(out=rows(xc[q][0:p, :]), in0=per_row(stat[0:p, q, :]), scalar=-1.0 / D,
                                       in1=rows(xin[q][0:p, :]), op0=ALU.mult, op1=ALU.add)\
                 .then_inc(S_center.sem, 1)

            def hidden(s, q, st, sq_st, p, tile):
                sq_st.done(dve, s)
                V.tensor_reduce(stat[0:p, 2, :], rows(sq[0:p, :]), AX, ALU.add).then_inc(st.sem, 1)
                st.part(dve, s, 1)
                inverse_sqrt(stat[0:p, 2, :], (stat[0:p, 3, :], stat[0:p, 4, :], stat[0:p, 5, :]),
                             1.0 / D, LN_EPS, st, s, 1)
                V.scalar_tensor_tensor(out=rows(tile), in0=rows(tile), scalar=0.0,
                                       in1=per_row(stat[0:p, 4, :]), op0=ALU.max, op1=ALU.mult)\
                 .then_inc(st.sem, 1)

            def h_ready(s, q, p=P):
                hidden(s, q, S_h, S_sq, p, xc[q][0:p, :])

            def edge_center(g, half, q):
                S_eg.done(dve, half, q)
                S_et.done(dve, g - 1)
                V.tensor_reduce(estat[:, 0, :], rows(eg[q][:, :]), AX, ALU.add).then_inc(S_ea.sem, 1)
                S_ea.part(dve, g, 1)
                V.scalar_tensor_tensor(out=rows(ec[:, :]), in0=per_row(estat[:, 0, :]), scalar=-1.0 / D,
                                       in1=rows(eg[q][:, :]), op0=ALU.mult, op1=ALU.add)\
                 .then_inc(S_ea.sem, 1)

            def edge_score(g):
                S_esq.done(dve, g)
                V.tensor_reduce(estat[:, 1, :], rows(esq[:, :]), AX, ALU.add).then_inc(S_eb.sem, 1)
                S_eb.part(dve, g, 1)
                inverse_sqrt(estat[:, 1, :], (estat[:, 2, :], estat[:, 3, :], estat[:, 4, :]),
                             1.0 / D, LN_EPS, S_eb, g, 1)
                V.scalar_tensor_tensor(out=rows(ec[:, :]), in0=rows(ec[:, :]), scalar=0.0,
                                       in1=per_row(estat[:, 3, :]), op0=ALU.max, op1=ALU.mult)\
                 .then_inc(S_eb.sem, 1)
                S_eb.part(dve, g, NEWTON + 3)
                V.tensor_tensor(prod[:, :], ec[:, 0:EJ * D], ec[:, EJ * D:2 * EJ * D], ALU.mult)\
                 .then_inc(S_eb.sem, 1)
                S_eb.part(dve, g, NEWTON + 4)
                V.tensor_reduce(score[:, :], rows(prod[:, :]), AX, ALU.add).then_inc(S_eb.sem, 1)

            def edge_weight(g):
                S_exp.done(dve, g)
                V.tensor_tensor(weighted[:, :, 0:D], rows(ec[:, 0:EJ * D]), per_row(weighted[:, :, D]),
                                ALU.mult).then_inc(S_ew.sem, 1)

            def edge_scan(g, half, q):
                S_et.done(dve, g)
                S_same.done(dve, half, q)
                S_agg.done(dve, g - 2)
                if isinstance(g, int) and g == 0:
                    carry = 0.0
                else:
                    S_scan.done(dve, g - 1)
                    carry = sums[1 - q][:, EG - 1:EG]
                V.tensor_tensor_scan(sums[q][:, :], same[q][0:D + 1, :], bank_w[0:D + 1, 0:EG], carry,
                                     ALU.mult, ALU.add).then_inc(S_scan.sem, 1)

            def edge_finish(g):
                S_agg.done(dve, g)
                S_rd.done(dve, g)
                S_es.done(dve, g - 1)
                acc = bank_a[0:EP, 0:EJ * (D + 1)].rearrange("p (j d) -> p j d", d=D + 1)
                V.reciprocal(inv[:, :], acc[:, :, D]).then_inc(S_ee.sem, 1)
                S_ee.part(dve, g, 1)
                V.tensor_tensor(diff[:, :, 0:D], acc[:, :, 0:D], per_row(inv[:, :]), ALU.mult)\
                 .then_inc(S_ee.sem, 1)
                S_ee.part(dve, g, 2)
                here = group_cols(dst_rows, g)
                V.tensor_tensor(rows(here), diff[:, :, 0:D], rows(rdst[:, :]), ALU.add).then_inc(S_ee.sem, 1)
                S_ee.part(dve, g, 3)
                V.tensor_tensor(twice[:, :], here, rdst[:, :], ALU.add).then_inc(S_ee.sem, 1)
                S_ee.part(dve, g, 4)
                V.tensor_tensor(diff[:, :, D:2 * D], diff[:, :, 0:D], rows(twice[:, :]), ALU.mult)\
                 .then_inc(S_ee.sem, 1)

            def half_body(it, k, dense, first=False):
                g, s = it * 2 + k, it * 4 + 2 * k
                if dense:
                    center(s, it * 2 + k, 0)
                edge_center(g, it, k)
                if dense and not first:
                    h_ready(s - 1, 1)
                if not first:
                    edge_scan(g - 1, it if k else it - 1, 1 - k)
                edge_score(g)
                if dense:
                    center(s + 1, it * 2 + k, 1)
                if not first:
                    edge_finish(g - 1)
                edge_weight(g)
                if dense:
                    h_ready(s, 0)

            half_body(0, 0, True, True)
            half_body(0, 1, True)
            with dve.Fori(1, BODY) as it:
                half_body(it, 0, True)
                half_body(it, 1, True)
            center(NS, NS // 2, 0, PT)
            h_ready(NS - 1, 1)
            h_ready(NS, 0, PT)
            with dve.Fori(BODY, GB) as it:
                half_body(it, 0, False)
                half_body(it, 1, False)
            edge_scan(G - 1, GB - 1, 1)
            edge_finish(G - 1)

            S_gram.done(dve, NS)
            S_es.done(dve, G)
            c = [1]

            def link(ins):
                c[0] += 1
                ins.then_inc(s_bnd, 1)
                dve.wait_ge(s_bnd, c[0])

            link(V.tensor_tensor(bndiag[:, :], bank_sum[:, 0:P], ident[:, :], ALU.mult))
            link(V.tensor_reduce(bncol[:, 0:1], bndiag[:, :], AX, ALU.add))
            link(V.tensor_copy(bncol[:, 1:3], bank_sum[:, P:P + 2]))
            link(V.tensor_tensor(bndiag[:, 0:D], ident[:, 0:D], ident[:, D:P], ALU.add))
            link(V.tensor_scalar(bnz[:, 0, 0, :], bndiag[:, 0:D], bncol[:, 1:2], None, ALU.mult))
            link(V.tensor_scalar(bnz[:, 0, 1, :], bndiag[:, 0:D], bncol[:, 0:1], None, ALU.mult))
            link(V.tensor_scalar(bnz[:, 1, :, :].rearrange("p a d -> p (a d)"), ident[:, :], bncol[:, 2:3],
                                 None, ALU.mult))
            bn_ready = c[0]
            assert bn_ready == 8
            dve.wait_ge(s_bnp, 1)
            mean, m2, var, v_, y_, a_, tmp = (bnw[:, i, :] for i in range(7))
            link(V.tensor_scalar(bnw[:, 0:2, :].rearrange("p a d -> p (a d)"), bank_r[0][:, 0:2 * D], 1.0 / N,
                                 None, ALU.mult))
            link(V.tensor_tensor(tmp, mean, mean, ALU.mult))
            link(V.tensor_tensor(var, m2, tmp, ALU.subtract))
            base = Stage(s_bnd, 0)

            class Linked:
                sem = s_bnd

                @staticmethod
                def part(eng, step, k):
                    eng.wait_ge(s_bnd, step + k)

            inverse_sqrt(var, (v_, y_, a_), 1.0, BN_EPS, Linked, c[0], 0)
            c[0] += NEWTON + 1
            link(V.tensor_tensor(bn[:, 0, :], bn_in[:, 0, :], y_, ALU.mult))
            link(V.tensor_tensor(tmp, mean, bn[:, 0, :], ALU.mult))
            link(V.tensor_tensor(bn[:, 1, :], bn_in[:, 1, :], tmp, ALU.subtract))

            def x2_center(s, half, q, p=P):
                L_x.done(dve, half, q)
                L_t.done(dve, s - 2)
                L_st.done(dve, half - 1, q)
                t_ = rows(x2[q][0:p, :])
                V.tensor_tensor(t_, rows(rin[q][0:p, :]), cols(bn[0:p, 0, :], R), ALU.mult).then_inc(L_f.sem, 1)
                L_f.part(dve, s, 1)
                V.tensor_tensor(x2[q][0:p, :], x2[q][0:p, :], xin[q][0:p, :], ALU.add).then_inc(L_f.sem, 1)
                L_f.part(dve, s, 2)
                V.tensor_tensor(t_, t_, cols(bn[0:p, 1, :], R), ALU.add).then_inc(L_f.sem, 1)
                L_f.part(dve, s, 3)
                V.tensor_reduce(stat[0:p, q, :], t_, AX, ALU.add).then_inc(L_f.sem, 1)
                L_f.part(dve, s, 4)
                V.scalar_tensor_tensor(out=rows(xc[q][0:p, :]), in0=per_row(stat[0:p, q, :]), scalar=-1.0 / D,
                                       in1=t_, op0=ALU.mult, op1=ALU.add).then_inc(L_f.sem, 1)

            def h2_ready(s, q, p=P):
                hidden(s, q, L_g, L_sq, p, xc[q][0:p, :])
                L_g.part(dve, s, NEWTON + 3)
                V.tensor_tensor(x2[q][0:p, :], x2[q][0:p, :], xc[q][0:p, :], ALU.add).then_inc(L_g.sem, 1)

            def final_rows(s, q, p=P):
                L_og.done(dve, s)
                L_g.done(dve, s)
                V.tensor_tensor(x2[q][0:p, :], x2[q][0:p, :], res[q][0:p, :], ALU.add).then_inc(L_y.sem, 1)

            def edge_x2(g, half, q):
                M_ld.done(dve, half, q)
                M_er.done(dve, half, q)
                M_t.done(dve, g - 1)
                V.tensor_tensor(rows(ex[:, :]), rows(er[q][:, :]), cols(bn[0:EP, 0, :], 2 * EJ), ALU.mult)\
                 .then_inc(M_a.sem, 1)
                M_a.part(dve, g, 1)
                V.tensor_tensor(ex[:, :], ex[:, :], eg[q][:, :], ALU.add).then_inc(M_a.sem, 1)
                M_a.part(dve, g, 2)
                V.tensor_tensor(rows(ex[:, :]), rows(ex[:, :]), cols(bn[0:EP, 1, :], 2 * EJ), ALU.add)\
                 .then_inc(M_a.sem, 1)
                M_a.part(dve, g, 3)
                V.tensor_reduce(estat[:, 0, :], rows(ex[:, :]), AX, ALU.add).then_inc(M_a.sem, 1)
                M_a.part(dve, g, 4)
                V.scalar_tensor_tensor(out=rows(ec[:, :]), in0=per_row(estat[:, 0, :]), scalar=-1.0 / D,
                                       in1=rows(ex[:, :]), op0=ALU.mult, op1=ALU.add).then_inc(M_a.sem, 1)

            def edge_h2(g, q):
                M_sq.done(dve, g)
                w = EJ * D
                V.tensor_reduce(estat[:, 1, :], rows(esq[:, :]), AX, ALU.add).then_inc(M_b.sem, 1)
                M_b.part(dve, g, 1)
                inverse_sqrt(estat[:, 1, :], (estat[:, 2, :], estat[:, 3, :], estat[:, 4, :]),
                             1.0 / D, LN_EPS, M_b, g, 1)
                V.scalar_tensor_tensor(out=hsrc[q][:, :, 0:D], in0=rows(ec[:, 0:w]), scalar=0.0,
                                       in1=per_row(estat[:, 3, 0:EJ]), op0=ALU.max, op1=ALU.mult)\
                 .then_inc(M_b.sem, 1)
                V.scalar_tensor_tensor(out=rows(hdst[:, :]), in0=rows(ec[:, w:2 * w]), scalar=0.0,
                                       in1=per_row(estat[:, 3, EJ:2 * EJ]), op0=ALU.max, op1=ALU.mult)\
                 .then_inc(M_b.sem, 1)
                M_b.part(dve, g, NEWTON + 4)
                V.tensor_tensor(group_cols(dst_rows, g), ex[:, w:2 * w], hdst[:, :], ALU.add)\
                 .then_inc(M_b.sem, 1)

            def edge_scan2(g, half, q):
                M_g2.done(dve, g)
                M_same.done(dve, half, q)
                M_c.done(dve, g - 2)
                if isinstance(g, int) and g == 0:
                    carry = 0.0
                else:
                    M_scan.done(dve, g - 1)
                    carry = pairT[1 - q][D:P, EG - 1:EG]
                V.tensor_tensor_scan(pairT[q][D:P, :], same[q][D:P, :], m2T[D:P, :], carry,
                                     ALU.mult, ALU.add).then_inc(M_scan.sem, 1)

            def edge_final(g):
                M_og.done(dve, g)
                here = group_cols(dst_rows, g)
                V.tensor_tensor(here, here, eadd[:, :], ALU.add).then_inc(M_y.sem, 1)

            def half_body2(it, k, dense, first=False):
                g, s = it * 2 + k, it * 4 + 2 * k
                if dense:
                    x2_center(s, it * 2 + k, 0)
                edge_x2(g, it, k)
                if dense and not first:
                    h2_ready(s - 1, 1)
                if not first:
                    edge_final(g - 1)
                edge_h2(g, k)
                if dense:
                    if not first:
                        final_rows(s - 1, 1)
                    x2_center(s + 1, it * 2 + k, 1)
                    h2_ready(s, 0)
                edge_scan2(g, it, k)
                if dense:
                    final_rows(s, 0)

            half_body2(0, 0, True, True)
            half_body2(0, 1, True)
            with dve.Fori(1, BODY) as it:
                half_body2(it, 0, True)
                half_body2(it, 1, True)
            h2_ready(NS - 1, 1)
            x2_center(NS, NS // 2, 0, PT)
            final_rows(NS - 1, 1)
            h2_ready(NS, 0, PT)
            final_rows(NS, 0, PT)
            with dve.Fori(BODY, GB) as it:
                half_body2(it, 0, False)
                half_body2(it, 1, False)
            edge_final(G - 1)

        @block.scalar
        def _(act):
            A = nc.scalar

            def square(s, q, p=P):
                S_center.done(act, s)
                S_h.done(act, s - 1)
                A.activation(sq[0:p, :], xc[q][0:p, :], ACT.Square).then_inc(S_sq.sem, 1)

            def products(s, q, p=P):
                for b in range(2):
                    S_t.part(act, s, b + 1)
                    S_r.done(act, s - 1)
                    A.activation(hT[:, b * 512:b * 512 + 512].rearrange("f (k n) -> f k n", n=P)[:, :, 0:p],
                                 bank_t[b][:, :].rearrange("f (k n) -> f k n", n=P)[:, :, 0:p],
                                 ACT.Copy).then_inc(S_ht.sem, 1)
                for b in range(2):
                    S_r.part(act, s, b + 1)
                    if b == 0:
                        S_gram.done(act, s - 2)
                        if isinstance(s, int):
                            S_st.done(act, s // 2 - 1, q)
                        else:
                            act.wait_ge(S_st.sems[q], store_count[0])
                    A.activation(res[q][0:p, b * 512:b * 512 + 512], bank_r[b][0:p, :], ACT.Relu)\
                     .then_inc(S_relu.sem, 1)

            store_count = [None]

            def edge_square(g):
                S_ea.done(act, g)
                S_eb.done(act, g - 1)
                A.activation(esq[:, :], ec[:, :], ACT.Square).then_inc(S_esq.sem, 1)

            def edge_exp(g):
                S_eb.done(act, g)
                S_et.done(act, g - 1)
                A.activation(weighted[:, :, D], score[:, :], ACT.Exp, bias=shift[0:EP, :])\
                 .then_inc(S_exp.sem, 1)

            def copy_hdT(g):
                S_et.done(act, g)
                S_agg.done(act, g - 1)
                A.activation(hdT[:, :], bank_d[0:D, 0:EG], ACT.Copy).then_inc(S_hd.sem, 1)

            def relu_dst(g):
                S_agg.done(act, g)
                S_ee.done(act, g - 1)
                A.activation(rdst[:, :], bank_d[0:EP, 0:EJ * D], ACT.Relu).then_inc(S_rd.sem, 1)

            def dense_products(s, half, q, p=P):
                store_count[0] = None if isinstance(s, int) else half * 16
                products(s, q, p)

            def half_body(it, k, dense, first=False):
                g, s = it * 2 + k, it * 4 + 2 * k
                if dense:
                    square(s, 0)
                edge_square(g)
                if dense and not first:
                    dense_products(s - 1, it * 2 + k - 1, 1)
                if not first:
                    relu_dst(g - 1)
                edge_exp(g)
                if dense:
                    square(s + 1, 1)
                copy_hdT(g)
                if dense:
                    dense_products(s, it * 2 + k, 0)

            act.wait_ge(s_v, 1)
            half_body(0, 0, True, True)
            half_body(0, 1, True)
            with act.Fori(1, BODY) as it:
                half_body(it, 0, True)
                half_body(it, 1, True)
            square(NS, 0, PT)
            products(NS - 1, 1)
            products(NS, 0, PT)
            with act.Fori(BODY, GB) as it:
                half_body(it, 0, False)
                half_body(it, 1, False)
            relu_dst(G - 1)

            act.wait_ge(s_w, 16 * 23)

            def square2(s, q, p=P):
                L_f.done(act, s)
                L_g.done(act, s - 1)
                A.activation(sq[0:p, :], xc[q][0:p, :], ACT.Square).then_inc(L_sq.sem, 1)

            def mlp(s, q, p=P):
                for b in range(2):
                    L_t.part(act, s, b + 1)
                    L_c.done(act, s - 1)
                    A.activation(hT[:, b * 512:b * 512 + 512].rearrange("f (k n) -> f k n", n=P)[:, :, 0:p],
                                 bank_h[:, :].rearrange("f (k n) -> f k n", n=P)[:, :, 0:p],
                                 ACT.Copy).then_inc(L_ht.sem, 1)
                for b in range(2):
                    L_c.part(act, s, b + 1)
                    if b:
                        L_o.part(act, s, b)
                    else:
                        L_o.done(act, s - 1)
                    for h in range(2):
                        ins = A.activation(cT[:, h, :].rearrange("f (k n) -> f k n", n=P)[:, :, 0:p],
                                           bank_c[h][0:H2, :].rearrange("f (k n) -> f k n", n=P)[:, :, 0:p],
                                           ACT.Gelu, bias=bc1[:, :])
                    ins.then_inc(L_cg.sem, 1)
                    L_o.part(act, s, b + 1)
                    if b == 0:
                        L_y.done(act, s - 2)
                    A.activation(res[q][0:p, b * 512:b * 512 + 512], bank_o[0:p, :], ACT.Gelu)\
                     .then_inc(L_og.sem, 1)

            def edge_square2(g):
                M_a.done(act, g)
                M_b.done(act, g - 1)
                A.activation(esq[:, :], ec[:, :], ACT.Square).then_inc(M_sq.sem, 1)

            def edge_message(g, q):
                M_t.done(act, g)
                M_m1.done(act, g - 1)
                A.activation(restT[:, :], bank_e2[0:D + DE, 0:EG], ACT.Copy).then_inc(M_tc.sem, 1)
                M_c.done(act, g - 2)
                A.activation(pairT[q][0:D, :], bank_e1[0:D, 0:EG], ACT.Copy).then_inc(M_tc.sem, 1)
                M_m1.done(act, g)
                M_m2.done(act, g - 1)
                A.activation(m1T[:, :], bank_m[0:H1, 0:EG], ACT.Gelu, bias=bm1[:, :]).then_inc(M_g1.sem, 1)
                M_m2.done(act, g)
                M_scan.done(act, g - 1)
                A.activation(m2T[D:P, :], bank_q[D:P, 0:EG], ACT.Gelu, bias=bm2[D:P, :]).then_inc(M_g2.sem, 1)

            def edge_combine(g):
                M_c.done(act, g)
                M_o.done(act, g - 1)
                A.activation(ecT[:, :], bank_m[0:H2, 0:EG], ACT.Gelu, bias=bc1[:, :]).then_inc(M_cg.sem, 1)
                M_o.done(act, g)
                M_y.done(act, g - 1)
                A.activation(eadd[:, :], bank_q[0:EP, 0:EJ * D], ACT.Gelu).then_inc(M_og.sem, 1)

            def half_body2(it, k, dense, first=False):
                g, s = it * 2 + k, it * 4 + 2 * k
                if dense:
                    square2(s, 0)
                edge_square2(g)
                if dense and not first:
                    mlp(s - 1, 1)
                if dense:
                    square2(s + 1, 1)
                edge_message(g, k)
                if dense:
                    mlp(s, 0)
                edge_combine(g)

            half_body2(0, 0, True, True)
            half_body2(0, 1, True)
            with act.Fori(1, BODY) as it:
                half_body2(it, 0, True)
                half_body2(it, 1, True)
            mlp(NS - 1, 1)
            square2(NS, 0, PT)
            mlp(NS, 0, PT)
            with act.Fori(BODY, GB) as it:
                half_body2(it, 0, False)
                half_body2(it, 1, False)

        @block.tensor
        def _(pe):
            T = nc.tensor
            pe.wait_ge(s_v, 15)
            pe.wait_ge(s_c, 2)
            pe.wait_ge(s_w, 16 * 23)
            b_res = bias16[:, 0, :, :].rearrange("p r d -> p (r d)")
            b_out = bias16[:, 1, :, :].rearrange("p r d -> p (r d)")
            def zero_sums(start, stop):
                return T.matmul(bank_sum[:, :], wm2[:, 0:1].broadcast_to([H1, P]),
                                ones[0:H1, 0:1].broadcast_to([H1, 512]), start=start, stop=stop)

            zero_sums(True, False).then_inc(s_zero, 1)

            def transposes(s, q, st, ready, copied, banks, p):
                ready.done(pe, s)
                for b in range(2):
                    if banks[0] is banks[1] and b:
                        copied.part(pe, s, 1)
                    else:
                        copied.done(pe, s - 1)
                    for k in range(4):
                        c = (4 * b + k) * P
                        ins = T.transpose(banks[b][:, k * P:k * P + p], xc[q][0:p, c:c + P], ident[0:p, 0:p])
                    ins.then_inc(st.sem, 1)

            def add_sums(s, q, p=P):
                S_relu.done(pe, s)
                for k in range(PAIRS):
                    r_ = res[q][0:p, k * P:k * P + P]
                    T.matmul(bank_sum[:, 0:P], r_, r_, start=False, stop=False)
                    ins = T.matmul(bank_sum[:, P:P + 1], r_, ones[0:p, 0:1], start=False, stop=False)
                ins.then_inc(S_gram.sem, 1)

            def r_products(s, q, p=P):
                for b in range(2):
                    S_ht.part(pe, s, b + 1)
                    S_relu.done(pe, s - 1)
                    for k in range(4):
                        c = (4 * b + k) * P
                        T.matmul(bank_r[b][0:p, k * P:k * P + P], hT[:, c:c + p], wres2[:, :],
                                 start=(k == 0), stop=False)
                    T.matmul(bank_r[b][0:p, :], ones16[:, 0:p], b_res, start=False, stop=True)\
                     .then_inc(S_r.sem, 1)

            def dense1(s, q, p=P):
                transposes(s, q, S_t, S_h, S_ht, bank_t, p)
                if not (isinstance(s, int) and s == 0):
                    add_sums(s - 1, 1 - q)
                r_products(s, q, p)

            def edge_transposes(g):
                S_ew.done(pe, g)
                S_scan.done(pe, g - 1)
                S_rd.done(pe, g - 1)
                for j in range(EJ):
                    T.transpose(bank_w[0:D + 1, j:EG:EJ], weighted[:, j, :], ident[0:EP, 0:EP])
                    ins = T.transpose(bank_d[0:D, j:EG:EJ], ec[:, (EJ + j) * D:(EJ + j + 1) * D],
                                      ident[0:EP, 0:EP])
                ins.then_inc(S_et.sem, 1)

            def edge_products(g, q):
                S_scan.done(pe, g)
                S_hd.done(pe, g)
                S_ee.done(pe, g - 1)
                for j in range(EJ):
                    ins = T.matmul(bank_a[0:EP, j * (D + 1):(j + 1) * (D + 1)], sums[q][:, j:EG:EJ],
                                   wconv[:, :], start=(j == 0), stop=(j == EJ - 1))
                ins.then_inc(S_agg.sem, 1)
                for j in range(EJ):
                    T.matmul(bank_d[0:EP, j * D:(j + 1) * D], hdT[:, j:EG:EJ], wres2[0:D, 0:D],
                             start=(j == 0), stop=False)
                T.matmul(bank_d[0:EP, 0:EJ * D], ones16[:, 0:EP], b_res[:, 0:EJ * D], start=False, stop=True)\
                 .then_inc(S_agg.sem, 1)

            def edge_stats(g):
                S_ee.done(pe, g)
                for j in range(EJ):
                    c = last[:, g * EJ + j:g * EJ + j + 1] if isinstance(g, int) else \
                        last[:, bass.ds(g * EJ + j, 1)]
                    ins = T.matmul(bank_sum[:, P + 1:P + 2], diff[:, j, :], c, start=False, stop=False)
                ins.then_inc(S_es.sem, 1)

            def half_body(it, k, dense, first=False):
                g, s = it * 2 + k, it * 4 + 2 * k
                if dense and not first:
                    dense1(s - 1, 1)
                if not first:
                    edge_products(g - 1, 1 - k)
                    edge_stats(g - 1)
                edge_transposes(g)
                if dense:
                    dense1(s, 0)

            pe.wait_ge(s_zero, 1)
            half_body(0, 0, True, True)
            half_body(0, 1, True)
            with pe.Fori(1, BODY) as it:
                half_body(it, 0, True)
                half_body(it, 1, True)
            dense1(NS - 1, 1)
            dense1(NS, 0, PT)
            add_sums(NS, 0, PT)
            with pe.Fori(BODY, GB) as it:
                half_body(it, 0, False)
                half_body(it, 1, False)
            edge_products(G - 1, 1)
            edge_stats(G - 1)
            zero_sums(False, True).then_inc(S_es.sem, 1)

            pe.wait_ge(s_bnd, 8)
            T.matmul(bank_r[0][:, 0:P], ones[:, :], bnz[:, 0, :, :].rearrange("p a d -> p (a d)"),
                     start=True, stop=False)
            T.matmul(bank_r[0][:, 0:P], ones[:, :], bnz[:, 1, :, :].rearrange("p a d -> p (a d)"),
                     start=False, stop=True).then_inc(s_bnp, 1)
            pe.wait_ge(s_bnd, 9)

            def dense2(s, q, p=P):
                transposes(s, q, L_t, L_g, L_ht, (bank_h, bank_h), p)
                for b in range(2):
                    L_ht.part(pe, s, b + 1)
                    if b:
                        L_cg.part(pe, s, b)
                    else:
                        L_cg.done(pe, s - 1)
                    for h in range(2):
                        o = bank_c[h][0:H2, :]
                        i = hT[h * D:h * D + D, b * 512:b * 512 + 512]
                        if p != P:
                            o = o.rearrange("f (k n) -> f k n", n=P)[:, :, 0:p]
                            i = i.rearrange("f (k n) -> f k n", n=P)[:, :, 0:p]
                        ins = T.matmul(o, wc1_node[h * D:h * D + D, :], i, start=True, stop=True)
                    ins.then_inc(L_c.sem, 1)
                    L_cg.part(pe, s, b + 1)
                    if b:
                        L_og.part(pe, s, b)
                    else:
                        L_og.done(pe, s - 1)
                    for k in range(4):
                        for h in range(2):
                            c = (2 * k + h) * D
                            T.matmul(bank_o[0:p, c:c + D], cT[:, h, k * P:k * P + p], wc2[:, :],
                                     start=(k == 0 and h == 0), stop=False)
                    T.matmul(bank_o[0:p, :], ones16[:, 0:p], b_out, start=False, stop=True)\
                     .then_inc(L_o.sem, 1)

            def edge_transposes2(g, q):
                M_b.done(pe, g)
                M_tc.done(pe, g - 1)
                for j in range(EJ):
                    ins = T.transpose(bank_e2[0:D + DE, j:EG:EJ], hsrc[q][:, j, :], ident[0:EP, 0:EP])
                ins.then_inc(M_t.sem, 1)
                for j in range(EJ):
                    ins = T.transpose(bank_e1[0:D, j:EG:EJ], hdst[:, j * D:j * D + D], ident[0:EP, 0:EP])
                ins.then_inc(M_t.sem, 1)

            def edge_messages(g, q):
                M_tc.done(pe, g)
                M_cg.done(pe, g - 1)
                T.matmul(bank_m[0:H1, 0:EG], wm1_rest[:, :], restT[:, :], start=True, stop=False)
                T.matmul(bank_m[0:H1, 0:EG], wm1_dst[:, :], pairT[q][0:D, :], start=False, stop=True)\
                 .then_inc(M_m1.sem, 1)
                M_g1.done(pe, g)
                M_og.done(pe, g - 1)
                T.matmul(bank_q[:, 0:EG], wm2[:, :], m1T[:, :], start=True, stop=True).then_inc(M_m2.sem, 1)

            def edge_combine(g, q):
                M_scan.done(pe, g)
                T.matmul(bank_m[0:H2, 0:EG], wc1[:, :], pairT[q][:, :], start=True, stop=True)\
                 .then_inc(M_c.sem, 1)
                M_cg.done(pe, g)
                M_g2.done(pe, g)
                for j in range(EJ):
                    T.matmul(bank_q[0:EP, j * D:(j + 1) * D], ecT[:, j:EG:EJ], wc2[:, :],
                             start=(j == 0), stop=False)
                T.matmul(bank_q[0:EP, 0:EJ * D], ones16[:, 0:EP], b_out[:, 0:EJ * D], start=False, stop=True)\
                 .then_inc(M_o.sem, 1)

            def half_body2(it, k, dense, first=False):
                g, s = it * 2 + k, it * 4 + 2 * k
                if dense and not first:
                    dense2(s - 1, 1)
                edge_transposes2(g, k)
                edge_messages(g, k)
                if dense:
                    dense2(s, 0)
                edge_combine(g, k)

            half_body2(0, 0, True, True)
            half_body2(0, 1, True)
            with pe.Fori(1, BODY) as it:
                half_body2(it, 0, True)
                half_body2(it, 1, True)
            dense2(NS - 1, 1)
            dense2(NS, 0, PT)
            with pe.Fori(BODY, GB) as it:
                half_body2(it, 0, False)
                half_body2(it, 1, False)


_INS = ["x", "src", "dst", "edge_attr_32", "L0_gnn_W_conv", "L0_gnn_b_conv", "L0_gnn_W_res", "L0_gnn_b_res",
        "L0_gnn_gamma", "L0_gnn_beta", "L1_gnn_W_m1", "L1_gnn_b_m1", "L1_gnn_W_m2", "L1_gnn_b_m2",
        "L1_gnn_W_c1", "L1_gnn_b_c1", "L1_gnn_W_c2", "L1_gnn_b_c2"]


def kernel(**inputs):
    import numpy as np
    import concourse.bacc as bacc
    from concourse.bass_utils import run_bass_kernel_spmd as run

    nc = bacc.Bacc("TRN2", target_bir_lowering=False, num_devices=1)
    arrays, aps = {}, {}
    for name in _INS:
        a = np.ascontiguousarray(inputs[name])
        arrays[f"in_{name}"] = a
        aps[name] = nc.dram_tensor(f"in_{name}", a.shape, mybir.dt.from_np(a.dtype), kind="ExternalInput").ap()
    out = nc.dram_tensor("out_0", arrays["in_x"].shape, F32, kind="ExternalOutput").ap()
    program(nc, aps, out)
    r = run(nc, [arrays], core_ids=[0])
    return r.results[0]["out_0"]
```

```python
from contextlib import ExitStack

import concourse.bass as bass
from concourse import mybir

F32 = mybir.dt.float32
BF16 = mybir.dt.bfloat16
I32 = mybir.dt.int32
ALU = mybir.AluOpType
ACT = mybir.ActivationFunctionType
AX = mybir.AxisListType.X

P = 128
D = 64
DE = 32
EP = 125
EJ = 4
EG = EP * EJ
R = 16
RD = R * D
PAIRS = R // 2
STEP = P * R
LN_EPS = 1e-5
BN_EPS = 1e-5
SHIFT = 32.0
BEYOND = 1048576
MAGIC = float(0x5F3759DF)
NEWTON = 10
BN_PARTS = 8


class Stage:

    def __init__(self, sem, incs=1):
        self.sem, self.incs = sem, incs

    def done(self, eng, step):
        if isinstance(step, int) and step < 0:
            return
        eng.wait_ge(self.sem, step * self.incs + self.incs)

    def part(self, eng, step, k):
        if isinstance(step, int) and step < 0:
            return
        eng.wait_ge(self.sem, step * self.incs + k)


class Unit:

    def __init__(self, s, b, j, m, turn):
        self.s, self.b = s, b
        self.j, self.m = j, m
        self.turn = turn


class Slots:

    def __init__(self, sems, incs=16):
        self.sems, self.incs = sems, incs

    def done(self, eng, turn, q):
        if isinstance(turn, int) and turn < 0:
            return
        eng.wait_ge(self.sems[q], turn * self.incs + self.incs)


def program(nc, t, out):
    x, src, dst, ea = t["x"], t["src"], t["dst"], t["edge_attr_32"]
    N = x.shape[0]
    E = src.shape[0]
    G = E // EG
    NS = N // STEP
    PT = (N - NS * STEP) // R
    HD = NS // 2
    BODY = HD // 2
    GB = G // 2
    assert G * EG == E and NS % 4 == 0 and PT * R + NS * STEP == N and PT <= P and G % 2 == 0
    assert N < 1 << 20 and G == 2 * HD + 2 and G % 4 == 2
    H1 = t["L1_gnn_W_m1"].shape[1]
    H2 = t["L1_gnn_W_c1"].shape[1]

    with ExitStack() as ctx:
        def sb(name, shape, dt=F32):
            return ctx.enter_context(nc.sbuf_tensor(name, shape, dt))

        def pb(name):
            return ctx.enter_context(nc.psum_tensor(name, [P, 512], F32))

        def sem(name):
            return ctx.enter_context(nc.semaphore(name))

        def stage(name, incs=1):
            return Stage(sem(name), incs)

        def slots(name, incs=16, n=2):
            return Slots([sem(f"{name}{q}") for q in range(n)], incs)

        table = nc.dram_tensor("layer0_rows", (N, D), F32).ap()
        layer0_edge_rows = nc.dram_tensor("layer0_edge_rows", (G, EP, 2 * EJ * D), F32).ap()
        edge_rows = nc.dram_tensor("edge_rows", (G, EP, 2 * EJ * D), F32).ap()
        dst_pad = nc.dram_tensor("dst_pad", (E + 2,), I32).ap()
        same_row = nc.dram_tensor("same_row", (E,), F32).ap()
        put_row = nc.dram_tensor("put_row", (E,), I32).ap()

        ident = sb("ident", [P, P])
        ones = sb("ones", [P, P])
        ones16 = sb("ones16", [D + 1, P], BF16)
        shift = sb("shift", [P, 1])
        wres2 = sb("wres2", [P, P])
        wconv = sb("wconv", [D + 1, D + 1])
        bias_in = sb("bias_in", [D + 1, 2, D])
        bias_rest = sb("bias_rest", [D + 1, 2, 2, D])
        bias_part = sb("bias_part", [D + 1, 3, 2, D], BF16)
        bias16 = sb("bias16", [D + 1, 2, 8, D], BF16)
        wc1_node = sb("wc1_node", [P, H2])
        wc1 = sb("wc1", [P, H2])
        wc2 = sb("wc2", [H2, D])
        wm1_dst = sb("wm1_dst", [D, H1])
        wm1_rest = sb("wm1_rest", [D + DE, H1])
        wm2 = sb("wm2", [H1, P])
        bm1 = sb("bm1", [H1, 1])
        bm2 = sb("bm2", [P, 1])
        bc1 = sb("bc1", [H2, 1])
        bn_in = sb("bn_in", [P, 2, D])
        bn = sb("bn", [P, 2, D])

        dst_idx = sb("dst_idx", [EP, G * EJ], I32)
        next_idx = sb("next_idx", [EP, G * EJ], I32)
        put_idx = sb("put_idx", [EP, G * EJ], I32)
        get_idx = [sb(f"get_idx{q}", [EP, 2 * EJ], I32) for q in range(4)]
        put_now = [sb(f"put_now{i}", [EP, EJ], I32) for i in range(4)]
        put_rows = [sb(f"put_rows{i}", [EP, EJ * D]) for i in range(4)]
        last = sb("last", [EP, G * EJ])
        flat = sb("flat", [EP, 2, E // EP], I32)
        same_flat = sb("same_flat", [EP, E // EP])
        end_mark = sb("end_mark", [1, 2], I32)

        xin = [sb(f"xin{q}", [P, RD]) for q in range(2)]
        rin = [sb(f"rin{q}", [P, RD]) for q in range(2)]
        xc = [sb(f"xc{q}", [P, RD]) for q in range(4)]
        x2 = [sb(f"x2_{q}", [P, RD]) for q in range(4)]
        sq = [sb(f"sq{q}", [P, RD]) for q in range(2)]
        hT = sb("hT", [P, RD])
        res = [sb(f"res{q}", [P, RD]) for q in range(2)]
        cT = [sb(f"cT{b}", [H2, 2, 512]) for b in range(2)]
        stat = sb("stat", [P, 5, 2 * R + 2 * EJ])

        ring = [sb(f"ring{q}", [EP, 2 * EJ * D]) for q in range(4)]
        eg = [sb(f"eg{q}", [EP, 2 * EJ * D]) for q in range(2)]
        er = [sb(f"er{q}", [EP, 2 * EJ * D]) for q in range(2)]
        ec = [sb(f"ec{q}", [EP, 2 * EJ * D]) for q in range(2)]
        ex = sb("ex", [EP, 2 * EJ * D])
        esq = sb("esq", [EP, 2 * EJ * D])
        prod = sb("prod", [EP, EJ * D])
        score = sb("score", [EP, EJ])
        weighted = sb("weighted", [EP, EJ, D + 1])
        same = [sb(f"same{q}", [P, EG]) for q in range(2)]
        sums = [sb(f"sums{q}", [D + 1, EG]) for q in range(2)]
        hdT = sb("hdT", [D, EG])
        rdst = sb("rdst", [EP, EJ * D])
        inv = sb("inv", [EP, EJ])
        diff = sb("diff", [EP, EJ, 2 * D])
        twice = sb("twice", [EP, EJ * D])
        dst_rows = sb("dst_rows", [EP, G * EJ * D])
        hsrc = [sb(f"hsrc{q}", [EP, EJ, D + DE]) for q in range(2)]
        hdst = sb("hdst", [EP, EJ * D])
        restT = sb("restT", [D + DE, EG])
        m1T = sb("m1T", [H1, EG])
        m2T = sb("m2T", [P, EG])
        pairT = [sb(f"pairT{q}", [P, EG]) for q in range(2)]
        ecT = sb("ecT", [H2, EG])
        eadd = sb("eadd", [EP, EJ * D])

        bnz = sb("bnz", [P, 2, 2, D])
        bncol = sb("bncol", [P, 4])
        bndiag = sb("bndiag", [P, P])
        bnw = sb("bnw", [P, 8, D])

        B = [pb(f"bank{i}") for i in range(8)]
        bank_t, bank_r, bank_sum = B[0:2], B[2:4], B[4]
        bank_w, bank_d, bank_a = B[5], B[6], B[7]
        bank_h, bank_c, bank_o = B[0], (B[1:3], B[3:5]), B[5]
        bank_x, bank_y = B[6], B[7]

        s_w = sem("weights_loaded")
        s_dst = sem("dst_loaded")
        s_pad = sem("dst_padded")
        s_flat = sem("dst_windows_loaded")
        s_sameput = sem("same_row_stored")
        s_puts = sem("put_row_stored")
        s_c = sem("pool_constants")
        s_v = sem("vector_setup")
        s_zero = sem("sums_bank_cleared")
        S_ix = slots("get_idx_loaded", 32, 4)
        S_get = slots("x_gathered", 16 * 2 * EJ, 4)
        S_stash = slots("x_stashed", 16, 4)
        S_eg = slots("edge_x_loaded")
        S_same = slots("same_loaded")
        S_px = slots("put_loaded", 32, 4)
        S_put = slots("layer0_rows_scattered", 16 * EJ, 4)
        S_x = slots("x_loaded")
        S_st = slots("r_stored")
        S_center = stage("centered", 2)
        S_sq = stage("squared")
        S_ss = stage("squares_summed")
        S_inv = stage("deviations_inverted", NEWTON + 1)
        S_h = stage("h_ready")
        S_t = stage("h_transposed", 2)
        S_ht = stage("hT_copied", 2)
        S_r = stage("r_product", 2)
        S_relu = stage("r_ready", 2)
        S_gram = stage("r_summed", 2)
        S_ea = stage("edge_centered", 2)
        S_esq = stage("edge_squared")
        S_ess = stage("edge_squares_summed")
        S_eb = stage("edge_scored", 3)
        S_exp = stage("edge_exp")
        S_ew = stage("edge_weighted")
        S_et = stage("edge_transposed")
        S_hd = stage("hdT_copied")
        S_scan = stage("segment_summed")
        S_agg = stage("edge_products", 2)
        S_rd = stage("r_of_dst")
        S_ee = stage("dst_row_ready", 5)
        S_es = stage("edge_stats_added")
        s_first = sem("first_group_stashed")
        s_bnp = sem("bn_summed")
        s_bnd = sem("bn_vector")
        L_ix = slots("get_idx_reloaded", 32, 4)
        L_get = slots("layer0_rows_gathered", 16 * 2 * EJ, 4)
        L_stash = slots("layer0_rows_stashed", 16, 4)
        M_ld = slots("edge_rows_loaded", 48)
        M_same = slots("same_reloaded")
        L_px = slots("final_put_loaded", 32, 4)
        L_put = slots("final_rows_scattered", 16 * EJ, 4)
        L_x = slots("rows_loaded", 32)
        L_st = slots("final_rows_stored")
        L_f = stage("x2_centered", 5)
        L_sq = stage("x2_squared")
        L_ss = stage("x2_squares_summed")
        L_inv = stage("x2_deviations_inverted", NEWTON + 1)
        L_h = stage("h2_ready")
        L_yy = stage("x2_plus_h2")
        L_t = stage("h2_transposed", 2)
        L_ht = stage("h2T_copied", 2)
        L_c = stage("c_product", 2)
        L_cg = stage("c_gelu", 2)
        L_o = stage("out_product", 2)
        L_og = stage("out_gelu", 2)
        L_y = stage("final_row_ready")
        M_a = stage("edge_x2_centered", 5)
        M_sq = stage("edge_x2_squared")
        M_ss = stage("edge_x2_squares_summed")
        M_b = stage("edge_h2_ready", 3)
        M_t = stage("edge_h2_transposed", 2)
        M_tc = stage("edge_h2T_copied", 2)
        M_m1 = stage("message1_product")
        M_g1 = stage("message1_gelu")
        M_m2 = stage("message2_product")
        M_g2 = stage("message2_gelu")
        M_scan = stage("messages_summed")
        M_c = stage("edge_c_product")
        M_cg = stage("edge_c_gelu")
        M_o = stage("edge_out_product")
        M_og = stage("edge_out_gelu")
        M_y = stage("dst_final_ready")

        main = NS * STEP

        def dense_rows(a, s, p):
            if p == P:
                v = a[0:main, :].rearrange("(s p r) d -> s p (r d)", p=P, r=R)
                return v[s, :, :] if isinstance(s, int) else v[bass.ds(s, 1), :, :].rearrange("a p n -> (a p) n")
            return a[main:N, :].rearrange("(p r) d -> p (r d)", r=R)

        def one(a, g):
            if isinstance(g, int):
                return a[g]
            v = a[bass.ds(g, 1)]
            return v.rearrange("a p n -> (a p) n") if len(v.shape) == 3 else v.rearrange("a n -> (a n)")

        def rows(a):
            return a.rearrange("p (r d) -> p r d", d=D)

        def per_row(a, n=D):
            return a.unsqueeze(2).broadcast_to([a.shape[0], a.shape[1], n])

        def cols(a, w):
            return a.unsqueeze(1).broadcast_to([a.shape[0], w, a.shape[1]])

        def group_cols(t2, g, w=EJ * D):
            return t2[:, bass.ds(g * w, w)] if not isinstance(g, int) else t2[:, g * w:g * w + w]

        def in_range(g):
            return not isinstance(g, int) or 0 <= g < G

        def halves(loop, half):
            for k in range(4):
                half(k // 2, k % 2, 2, 2 if k else 0)
            with loop(2, BODY) as it:
                half(it, 0, 2, 2)
                half(it, 1, 2, 2)
            half(BODY, 0, 1, 2)
            half(BODY, 1, 0, 1)
            with loop(BODY + 1, GB) as it:
                half(it, 0, 0, 0)
                half(it, 1, 0, 0)
            half(GB, 0, 0, 0)
            half(GB, 1, 0, 0)

        def unit(h, k, n):
            a = n // 2
            return Unit(s=h * 2 + (a - 2), b=n % 2, j=a % 2, m=(2 * k - 2 + a) % 4,
                                   turn=h + (a // 2 - 1))

        def in_work(u, n, before):
            if isinstance(u.s, int):
                return (0 <= u.s <= NS) and (before > 0)
            return before > 0

        def part_of(s):
            return PT if isinstance(s, int) and s == NS else P

        block = ctx.enter_context(nc.Block())

        @block.sync
        def _(sp):
            def load_small(dst_ap, src_ap):
                sp.dma_start(dst_ap, src_ap).then_inc(s_w, 16)

            def edge_values(a, g):
                return one(a.rearrange("(g p j) -> g p j", p=EP, j=EJ), g)

            def load_idx(g, q, loaded):
                sp.dma_start(get_idx[q][:, 0:EJ], edge_values(src, g)).then_inc(loaded.sems[q], 16)
                sp.dma_start(get_idx[q][:, EJ:2 * EJ], edge_values(dst, g)).then_inc(loaded.sems[q], 16)

            for g in range(4):
                load_idx(g, g, S_ix)
            sp.dma_start(dst_idx[:, :].rearrange("p (g j) -> p g j", j=EJ),
                         dst.rearrange("(g p j) -> p g j", p=EP, j=EJ)).then_inc(s_dst, 16)

            def col(a):
                return a.rearrange("(n a) -> n a", a=1)

            def row(a):
                return a.rearrange("(a n) -> a n", a=1)

            sp.wait_ge(s_v, 1)
            load_small(wres2[0:D, 0:D], t["L0_gnn_W_res"])
            load_small(wres2[D:P, D:P], t["L0_gnn_W_res"])
            load_small(wconv[0:D, 0:D], t["L0_gnn_W_conv"])
            load_small(wconv[D:D + 1, 0:D], row(t["L0_gnn_b_conv"]))
            for p in (0, 32, 64):
                load_small(bias_in[p:p + 1, 0, :], row(t["L0_gnn_b_res"]))
                load_small(bias_in[p:p + 1, 1, :], row(t["L1_gnn_b_c2"]))
            load_small(wc1_node[0:D, :], t["L1_gnn_W_c1"][0:D, :])
            load_small(wc1_node[D:P, :], t["L1_gnn_W_c1"][0:D, :])
            load_small(wc1[:, :], t["L1_gnn_W_c1"])
            load_small(wc2[:, :], t["L1_gnn_W_c2"])
            load_small(wm1_dst[:, :], t["L1_gnn_W_m1"][D:2 * D, :])
            load_small(wm1_rest[0:D, :], t["L1_gnn_W_m1"][0:D, :])
            load_small(wm1_rest[D:D + DE, :], t["L1_gnn_W_m1"][2 * D:2 * D + DE, :])
            load_small(wm2[:, D:P], t["L1_gnn_W_m2"])
            load_small(bm1[:, :], col(t["L1_gnn_b_m1"]))
            load_small(bm2[D:P, :], col(t["L1_gnn_b_m2"]))
            load_small(bc1[:, :], col(t["L1_gnn_b_c1"]))
            load_small(bn_in[:, 0, :], row(t["L0_gnn_gamma"]).broadcast_to([P, D]))
            load_small(bn_in[:, 1, :], row(t["L0_gnn_beta"]).broadcast_to([P, D]))

            sp.dma_start(dst_pad[1:E + 1], dst).then_inc(s_pad, 16)
            sp.dma_start(dst_pad[0:1].rearrange("(a n) -> a n", a=1), end_mark[:, 0:1]).then_inc(s_pad, 16)
            sp.dma_start(dst_pad[E + 1:E + 2].rearrange("(a n) -> a n", a=1),
                         end_mark[:, 1:2]).then_inc(s_pad, 16)
            sp.wait_ge(s_pad, 48)
            for k in range(2):
                sp.dma_start(flat[:, k, :], dst_pad[k:E + k].rearrange("(p c) -> p c", p=EP))\
                  .then_inc(s_flat, 16)
            sp.dma_start(next_idx[:, :].rearrange("p (g j) -> p g j", j=EJ),
                         dst_pad[2:E + 2].rearrange("(g p j) -> p g j", p=EP, j=EJ)).then_inc(s_flat, 16)
            sp.wait_ge(s_v, 3)
            sp.dma_start(same_row.rearrange("(p c) -> p c", p=EP), same_flat[:, :]).then_inc(s_sameput, 16)
            sp.wait_ge(s_v, 4)
            sp.dma_start(put_row.rearrange("(g p j) -> p g j", p=EP, j=EJ),
                         put_idx[:, :].rearrange("p (g j) -> p g j", j=EJ)).then_inc(s_puts, 16)
            sp.wait_ge(s_sameput, 16)
            sp.wait_ge(s_puts, 16)

            def stash(it, i, got, rows_dram, stashed, loaded, more):
                got.done(sp, it, i)
                sp.dma_start(one(rows_dram, it * 4 + i), ring[i][:, :]).then_inc(stashed.sems[i], 16)
                if more:
                    load_idx(it * 4 + (i + 4), i, loaded)

            def stashed_before(h, it, k, stashed):
                if not isinstance(h, int):
                    if it is not None:
                        stashed.done(sp, it - (1 - k), 0)
                        for i in range(1, 4):
                            stashed.done(sp, it - 1, i)
                elif h < 4:
                    stashed.done(sp, (h + 1) // 4, (h + 1) % 4)
                elif h == HD + 1:
                    for i in range(4):
                        stashed.done(sp, (G - 1 - i) // 4, i)

            def load_same(g, q, p0, p1, scanned, loaded):
                scanned.done(sp, g - 2)
                sp.dma_start(same[q][p0:p1, :], one(same_row.rearrange("(g n) -> g n", n=EG), g)
                             .unsqueeze(0).broadcast_to([p1 - p0, EG])).then_inc(loaded.sems[q], 16)

            def load_put(g, turn, i, ready, loaded, put):
                ready.done(sp, g)
                put.done(sp, turn - 1, i)
                sp.dma_start(put_now[i][:, :], edge_values(put_row, g)).then_inc(loaded.sems[i], 16)
                sp.dma_start(put_rows[i][:, :], group_cols(dst_rows, g)).then_inc(loaded.sems[i], 16)

            def load_puts(it, k, ready, loaded, put):
                for j in range(2):
                    i = (2 * k + 2 + j) % 4
                    load_put(it * 4 + (2 * k + j - 2 * HD - 2), it - (BODY + 1) + k, i, ready, loaded, put)

            def sync_halves(dense, edge, gets, puts):
                def half(it, k, steps, before):
                    h = it * 2 + k
                    dense(h, steps, before)
                    if steps:
                        for j in range(2):
                            if not isinstance(h, int) or h < HD or 2 * h + j < G:
                                stash(it, 2 * k + j, *gets, not isinstance(h, int) or 2 * h + j + 4 < G)
                    edge(h, it, k, steps > 0)
                    if not steps:
                        load_puts(it, k, *puts)

                for k in range(4):
                    half(k // 2, k % 2, 2, 2 if k else 0)
                with sp.Fori(2, BODY - 1) as it:
                    half(it, 0, 2, 2)
                    half(it, 1, 2, 2)
                half(BODY - 1, 0, 2, 2)
                half(BODY - 1, 1, 2, 2)
                half(BODY, 0, 1, 2)
                half(BODY, 1, 0, 1)
                with sp.Fori(BODY + 1, GB - 1) as it:
                    half(it, 0, 0, 0)
                    half(it, 1, 0, 0)
                half(GB - 1, 0, 0, 0)
                half(GB - 1, 1, 0, 0)

            def load_x(s, turn, j):
                S_center.done(sp, s - 2)
                p = part_of(s)
                sp.dma_start(xin[j][0:p, :], dense_rows(x, s, p)).then_inc(S_x.sems[j], 16)

            def store_r(s, j):
                S_relu.done(sp, s)
                p = part_of(s)
                sp.dma_start(dense_rows(table, s, p), res[j][0:p, :]).then_inc(S_st.sems[j], 16)

            def dense1(h, steps, before):
                if steps == 2:
                    for j in range(2):
                        if not isinstance(h, int) or 2 * h + 2 + j <= NS:
                            load_x(h * 2 + (2 + j), h + 1, j)
                for s, j in ((h * 2 - 3, 1), (h * 2 - 2, 0)):
                    if (steps or before) and not (isinstance(s, int) and s < 0):
                        store_r(s, j)

            def edge1(h, it, k, stashing):
                load_same(h, k, 0, D + 1, S_scan, S_same)
                if in_range(h + 1):
                    stashed_before(h, it if stashing else None, k, S_stash)
                    S_ea.done(sp, h - 1)
                    sp.dma_start(eg[1 - k][:, :], one(edge_rows, h + 1)).then_inc(S_eg.sems[1 - k], 16)

            load_x(0, 0, 0)
            load_x(1, 0, 1)
            S_get.done(sp, 0, 0)
            sp.dma_start(edge_rows[0], ring[0][:, :]).then_inc(s_first, 16)
            sp.wait_ge(s_first, 16)
            sp.dma_start(eg[0][:, :], edge_rows[0]).then_inc(S_eg.sems[0], 16)
            sync_halves(dense1, edge1, (S_get, edge_rows, S_stash, S_ix), (S_ee, S_px, S_put))

            for q in range(2):
                S_st.done(sp, (NS - q) // 2, q)
            for i in range(4):
                S_put.done(sp, (G - 1 - i) // 4, i)
                load_idx(i, i, L_ix)

            def load_rows(s, turn, j):
                L_f.done(sp, s - 2)
                p = part_of(s)
                sp.dma_start(xin[j][0:p, :], dense_rows(x, s, p)).then_inc(L_x.sems[j], 16)
                sp.dma_start(rin[j][0:p, :], dense_rows(table, s, p)).then_inc(L_x.sems[j], 16)

            def store_final(s, j):
                L_y.done(sp, s)
                p = part_of(s)
                sp.dma_start(dense_rows(out, s, p), res[j][0:p, :]).then_inc(L_st.sems[j], 16)

            def dense2(h, steps, before):
                for j in range(2):
                    s = h * 2 - 4 + j
                    if (steps or before) and not (isinstance(s, int) and s < 0):
                        store_final(s, j)
                if steps == 0 and before:
                    store_final(NS, 0)
                if steps == 2:
                    for j in range(2):
                        if not isinstance(h, int) or 2 * h + 2 + j <= NS:
                            load_rows(h * 2 + (2 + j), h + 1, j)

            def load_edges(g, q):
                M_a.done(sp, g - 2)
                sp.dma_start(eg[q][:, :], one(edge_rows, g)).then_inc(M_ld.sems[q], 16)
                sp.dma_start(er[q][:, :], one(layer0_edge_rows, g)).then_inc(M_ld.sems[q], 16)
                M_t.done(sp, g - 2)
                sp.dma_start(hsrc[q][:, :, D:D + DE],
                             one(ea.rearrange("(g p j) d -> g p (j d)", p=EP, j=EJ), g)
                             .rearrange("p (j d) -> p j d", d=DE)).then_inc(M_ld.sems[q], 16)

            def edge2(h, it, k, stashing):
                load_same(h, k, D, P, M_scan, M_same)
                if in_range(h + 1):
                    stashed_before(h, it if stashing else None, k, L_stash)
                    load_edges(h + 1, 1 - k)

            load_rows(0, 0, 0)
            load_rows(1, 0, 1)
            L_get.done(sp, 0, 0)
            sp.dma_start(layer0_edge_rows[0], ring[0][:, :]).then_inc(s_first, 16)
            sp.wait_ge(s_first, 32)
            load_edges(0, 0)
            sync_halves(dense2, edge2, (L_get, layer0_edge_rows, L_stash, L_ix), (M_y, L_px, L_put))
            for q in range(2):
                L_st.done(sp, (NS - q) // 2, q)
            for i in range(4):
                L_put.done(sp, (G - 1 - i) // 4, i)

        @block.gpsimd
        def _(pool):
            nc.gpsimd.memset(ident[:, :], 0.0).then_inc(s_c, 1)
            nc.gpsimd.memset(ones[:, :], 1.0)
            nc.gpsimd.memset(ones16[:, :], 1.0)
            pool.wait_ge(s_c, 1)
            nc.gpsimd.affine_select(out=ident[:, :], in_=ident[:, :], compare_op=ALU.not_equal, fill=1.0,
                                    base=0, pattern=[[-1, P]], channel_multiplier=1).then_inc(s_c, 1)
            limit = pool.to_reg(N - 1)
            nodes = pool.to_reg(N)

            def waits_end():
                pool.reg_add(limit, nodes, -1)

            def gather(turn, i, source, loaded, stashed, got):
                loaded.done(pool, turn, i)
                stashed.done(pool, turn - 1, i)
                waits_end()
                for j in range(2 * EJ):
                    nc.gpsimd.indirect_dma_start(ring[i][:, j * D:j * D + D], None, source[:, :],
                                                 bass.IndirectOffsetOnAxis(ap=get_idx[i][:, j:j + 1], axis=0),
                                                 bounds_check=limit, oob_is_err=False)\
                      .then_inc(got.sems[i], 16)

            def scatter(turn, i, target, loaded, put):
                loaded.done(pool, turn, i)
                waits_end()
                for j in range(EJ):
                    nc.gpsimd.indirect_dma_start(target[:, :],
                                                 bass.IndirectOffsetOnAxis(ap=put_now[i][:, j:j + 1], axis=0),
                                                 put_rows[i][:, j * D:j * D + D], None,
                                                 bounds_check=limit, oob_is_err=False).then_inc(put.sems[i], 16)

            def groups(do, *args):
                for i in range(4):
                    do(0, i, *args)
                with pool.Fori(1, G // 4) as turn:
                    for i in range(4):
                        do(turn, i, *args)
                for i in range(G % 4):
                    do(G // 4, i, *args)

            groups(gather, x, S_ix, S_stash, S_get)
            for q in range(2):
                S_st.done(pool, (NS - q) // 2, q)
            groups(scatter, table, S_px, S_put)
            for i in range(4):
                S_put.done(pool, (G - 1 - i) // 4, i)
            groups(gather, table, L_ix, L_stash, L_get)
            for q in range(2):
                L_st.done(pool, (NS - q) // 2, q)
            groups(scatter, out, L_px, L_put)

        @block.vector
        def _(dve):
            V = nc.vector

            def inverse_sqrt(total, tmp, n_mean, eps, done):
                v, y, a = tmp
                done(V.tensor_scalar(v, total, n_mean, eps, ALU.mult, ALU.add))
                done(V.tensor_scalar(y.bitcast(I32), v.bitcast(I32), -0.5, MAGIC, ALU.mult, ALU.add))
                for _ in range(3):
                    done(V.scalar_tensor_tensor(out=a, in0=y, scalar=-0.5, in1=y, op0=ALU.mult, op1=ALU.mult))
                    done(V.tensor_tensor(a, a, v, ALU.mult))
                    done(V.scalar_tensor_tensor(out=y, in0=a, scalar=1.5, in1=y, op0=ALU.add, op1=ALU.mult))

            def in_stage(st, step):
                k = [0]

                def done(ins):
                    k[0] += 1
                    ins.then_inc(st.sem, 1)
                    st.part(dve, step, k[0])
                return done

            V.memset(wres2[:, :], 0.0)
            V.memset(wconv[:, :], 0.0)
            V.memset(wm2[:, :], 0.0)
            V.memset(bias_in[:, :, :], 0.0)
            V.memset(bias16[:, :, :, :], 0.0)
            V.memset(stat[:, :, :], 1.0)
            V.memset(shift[:, :], -SHIFT)
            V.memset(end_mark[:, :], -1).then_inc(s_v, 1)
            dve.wait_ge(s_v, 1)
            dve.wait_ge(s_w, 16 * 23)
            V.memset(wconv[D:D + 1, D:D + 1], 1.0)
            V.tensor_copy(bias_part[:, 0, :, :], bias_in[:, :, :]).then_inc(s_v, 1)
            dve.wait_ge(s_v, 2)
            dve.wait_ge(s_flat, 48)
            V.tensor_tensor(same_flat[:, :], flat[:, 0, :], flat[:, 1, :], ALU.is_equal).then_inc(s_v, 1)
            V.tensor_tensor(last[:, :], dst_idx[:, :], next_idx[:, :], ALU.is_equal).then_inc(s_bnd, 1)
            dve.wait_ge(s_bnd, 1)
            dve.wait_ge(s_dst, 16)
            V.scalar_tensor_tensor(out=put_idx[:, :], in0=last[:, :], scalar=float(BEYOND), in1=dst_idx[:, :],
                                   op0=ALU.mult, op1=ALU.add).then_inc(s_v, 1)
            dve.wait_ge(s_v, 4)
            V.tensor_scalar(last[:, :], last[:, :], -1.0, 1.0, ALU.mult, ALU.add).then_inc(s_v, 1)
            for i in range(2):
                V.tensor_tensor(bias_rest[:, i, :, :], bias_in[:, :, :] if i == 0 else bias_rest[:, 0, :, :],
                                bias_part[:, i, :, :], ALU.subtract).then_inc(s_v, 1)
                dve.wait_ge(s_v, 6 + 2 * i)
                V.tensor_copy(bias_part[:, i + 1, :, :], bias_rest[:, i, :, :]).then_inc(s_v, 1)
                dve.wait_ge(s_v, 7 + 2 * i)
            for i in range(3):
                for b in range(2):
                    V.tensor_copy(bias16[32 * i:32 * i + 1, b, :, :],
                                  cols(bias_part[32 * i:32 * i + 1, i, b, :], 8)).then_inc(s_v, 1)

            def sum_squares(total, squares, squared, step, st):
                squared.done(dve, step)
                V.tensor_reduce(total, rows(squares), AX, ALU.add).then_inc(st.sem, 1)

            def invert(h, steps, dense_sums, edge_sums, st):
                if steps:
                    dense_sums.done(dve, h * 2 + (1 if steps == 2 else 0))
                    p, c = P, 0
                else:
                    p, c = EP, 2 * R
                if in_range(h):
                    edge_sums.done(dve, h)
                inverse_sqrt(stat[0:p, 1, c:], tuple(stat[0:p, i, c:] for i in (2, 3, 4)), 1.0 / D, LN_EPS,
                             in_stage(st, h))

            def subtract_mean(tile, source, total, st, step, k):
                V.tensor_reduce(total, rows(source), AX, ALU.add).then_inc(st.sem, 1)
                st.part(dve, step, k)
                V.scalar_tensor_tensor(out=rows(tile), in0=per_row(total), scalar=-1.0 / D, in1=rows(source),
                                       op0=ALU.mult, op1=ALU.add).then_inc(st.sem, 1)

            def relu_scale(tile, source, deviation, st):
                V.scalar_tensor_tensor(out=tile, in0=source, scalar=0.0, in1=per_row(deviation), op0=ALU.max,
                                       op1=ALU.mult).then_inc(st.sem, 1)

            def center(s, turn, j, m):
                S_x.done(dve, turn, j)
                S_t.done(dve, s - 4)
                p = part_of(s)
                subtract_mean(xc[m][0:p, :], xin[j][0:p, :], stat[0:p, 0, j * R:j * R + R], S_center, s, 1)

            def edge_center(g, it, k):
                S_eg.done(dve, it, k)
                S_et.done(dve, g - 2)
                subtract_mean(ec[k][:, :], eg[k][:, :], stat[0:EP, 0, 2 * R:], S_ea, g, 1)

            def edge_score(g, k):
                w = EJ * D
                relu_scale(rows(ec[k][:, :]), rows(ec[k][:, :]), stat[0:EP, 3, 2 * R:], S_eb)
                S_eb.part(dve, g, 1)
                V.tensor_tensor(prod[:, :], ec[k][:, 0:w], ec[k][:, w:2 * w], ALU.mult).then_inc(S_eb.sem, 1)
                S_eb.part(dve, g, 2)
                S_exp.done(dve, g - 1)
                V.tensor_reduce(score[:, :], rows(prod[:, :]), AX, ALU.add).then_inc(S_eb.sem, 1)

            def edge_weight(g, k):
                S_exp.done(dve, g)
                V.tensor_tensor(weighted[:, :, 0:D], rows(ec[k][:, 0:EJ * D]), per_row(weighted[:, :, D]),
                                ALU.mult).then_inc(S_ew.sem, 1)

            def edge_scan(g, turn, q):
                S_et.done(dve, g)
                S_same.done(dve, turn, q)
                S_agg.done(dve, g - 2)
                if isinstance(g, int) and g == 0:
                    carry = 0.0
                else:
                    S_scan.done(dve, g - 1)
                    carry = sums[1 - q][:, EG - 1:EG]
                V.tensor_tensor_scan(sums[q][:, :], same[q][0:D + 1, :], bank_w[0:D + 1, 0:EG], carry,
                                     ALU.mult, ALU.add).then_inc(S_scan.sem, 1)

            def edge_finish(g):
                S_agg.done(dve, g)
                S_rd.done(dve, g)
                S_es.done(dve, g - 1)
                acc = bank_a[0:EP, 0:EJ * (D + 1)].rearrange("p (j d) -> p j d", d=D + 1)
                V.reciprocal(inv[:, :], acc[:, :, D]).then_inc(S_ee.sem, 1)
                S_ee.part(dve, g, 1)
                V.tensor_tensor(diff[:, :, 0:D], acc[:, :, 0:D], per_row(inv[:, :]), ALU.mult)\
                 .then_inc(S_ee.sem, 1)
                S_ee.part(dve, g, 2)
                here = group_cols(dst_rows, g)
                V.tensor_tensor(rows(here), diff[:, :, 0:D], rows(rdst[:, :]), ALU.add).then_inc(S_ee.sem, 1)
                S_ee.part(dve, g, 3)
                V.tensor_tensor(twice[:, :], here, rdst[:, :], ALU.add).then_inc(S_ee.sem, 1)
                S_ee.part(dve, g, 4)
                V.tensor_tensor(diff[:, :, D:2 * D], diff[:, :, 0:D], rows(twice[:, :]), ALU.mult)\
                 .then_inc(S_ee.sem, 1)

            def half1(it, k, steps, before):
                h = it * 2 + k
                if steps:
                    center(h * 2, h, 0, 2 * k)
                if in_range(h - 1):
                    edge_weight(h - 1, 1 - k)
                if steps == 2:
                    center(h * 2 + 1, h, 1, 2 * k + 1)
                if in_range(h):
                    edge_center(h, it, k)
                for j in range(steps):
                    s = h * 2 + j
                    p = part_of(s)
                    sum_squares(stat[0:p, 1, j * R:j * R + R], sq[j][0:p, :], S_sq, s, S_ss)
                if in_range(h):
                    sum_squares(stat[0:EP, 1, 2 * R:], esq[:, :], S_esq, h, S_ess)
                    invert(h, steps, S_ss, S_ess, S_inv)
                for j in range(steps):
                    s = h * 2 + j
                    p = part_of(s)
                    t_ = rows(xc[2 * k + j][0:p, :])
                    relu_scale(t_, t_, stat[0:p, 3, j * R:j * R + R], S_h)
                if in_range(h):
                    edge_score(h, k)
                if in_range(h - 1):
                    edge_scan(h - 1, it - 1 + k, 1 - k)
                if in_range(h - 2):
                    edge_finish(h - 2)

            halves(dve.Fori, half1)

            S_es.done(dve, G)
            c = [1]

            def link(ins):
                c[0] += 1
                ins.then_inc(s_bnd, 1)
                dve.wait_ge(s_bnd, c[0])

            link(V.tensor_tensor(bndiag[:, :], bank_sum[:, 0:P], ident[:, :], ALU.mult))
            link(V.tensor_reduce(bncol[:, 0:1], bndiag[:, :], AX, ALU.add))
            link(V.tensor_copy(bncol[:, 1:3], bank_sum[:, P:P + 2]))
            link(V.tensor_tensor(bndiag[:, 0:D], ident[:, 0:D], ident[:, D:P], ALU.add))
            link(V.tensor_scalar(bnz[:, 0, 0, :], bndiag[:, 0:D], bncol[:, 1:2], None, ALU.mult))
            link(V.tensor_scalar(bnz[:, 0, 1, :], bndiag[:, 0:D], bncol[:, 0:1], None, ALU.mult))
            link(V.tensor_scalar(bnz[:, 1, :, :].rearrange("p a d -> p (a d)"), ident[:, :], bncol[:, 2:3],
                                 None, ALU.mult))
            assert c[0] == BN_PARTS
            dve.wait_ge(s_bnp, 1)
            mean, m2, var, v_, y_, a_, tmp = (bnw[:, i, :] for i in range(7))
            link(V.tensor_scalar(bnw[:, 0:2, :].rearrange("p a d -> p (a d)"), bank_r[0][:, 0:2 * D], 1.0 / N,
                                 None, ALU.mult))
            link(V.tensor_tensor(tmp, mean, mean, ALU.mult))
            link(V.tensor_tensor(var, m2, tmp, ALU.subtract))
            inverse_sqrt(var, (v_, y_, a_), 1.0, BN_EPS, link)
            link(V.tensor_tensor(bn[:, 0, :], bn_in[:, 0, :], y_, ALU.mult))
            link(V.tensor_tensor(tmp, mean, bn[:, 0, :], ALU.mult))
            link(V.tensor_tensor(bn[:, 1, :], bn_in[:, 1, :], tmp, ALU.subtract))

            def x2_center(tile, mid, row, xrow, n, total, st, step):
                p = tile.shape[0]
                V.tensor_tensor(rows(tile), rows(row), cols(bn[0:p, 0, :], n), ALU.mult).then_inc(st.sem, 1)
                st.part(dve, step, 1)
                V.tensor_tensor(tile, tile, xrow, ALU.add).then_inc(st.sem, 1)
                st.part(dve, step, 2)
                V.tensor_tensor(rows(tile), rows(tile), cols(bn[0:p, 1, :], n), ALU.add).then_inc(st.sem, 1)
                st.part(dve, step, 3)
                subtract_mean(mid, tile, total, st, step, 4)

            def dense_x2(s, turn, j, m):
                L_x.done(dve, turn, j)
                L_t.done(dve, s - 4)
                L_y.done(dve, s - 4)
                p = part_of(s)
                x2_center(x2[m][0:p, :], xc[m][0:p, :], rin[j][0:p, :], xin[j][0:p, :], R,
                          stat[0:p, 0, j * R:j * R + R], L_f, s)

            def edge_x2(g, it, k):
                M_ld.done(dve, it, k)
                M_b.done(dve, g - 1)
                x2_center(ex[:, :], ec[0][:, :], er[k][:, :], eg[k][:, :], 2 * EJ, stat[0:EP, 0, 2 * R:], M_a, g)

            def edge_h2(g, k):
                w = EJ * D
                M_t.done(dve, g - 1)
                relu_scale(hsrc[k][:, :, 0:D], rows(ec[0][:, 0:w]), stat[0:EP, 3, 2 * R:2 * R + EJ], M_b)
                relu_scale(rows(hdst[:, :]), rows(ec[0][:, w:2 * w]), stat[0:EP, 3, 2 * R + EJ:], M_b)
                M_b.part(dve, g, 2)
                V.tensor_tensor(group_cols(dst_rows, g), ex[:, w:2 * w], hdst[:, :], ALU.add)\
                 .then_inc(M_b.sem, 1)

            def edge_scan2(g, turn, q):
                M_g2.done(dve, g)
                M_same.done(dve, turn, q)
                M_c.done(dve, g - 2)
                if isinstance(g, int) and g == 0:
                    carry = 0.0
                else:
                    M_scan.done(dve, g - 1)
                    carry = pairT[1 - q][D:P, EG - 1:EG]
                V.tensor_tensor_scan(pairT[q][D:P, :], same[q][D:P, :], m2T[D:P, :], carry,
                                     ALU.mult, ALU.add).then_inc(M_scan.sem, 1)

            def edge_final(g):
                M_og.done(dve, g)
                M_b.done(dve, g)
                here = group_cols(dst_rows, g)
                V.tensor_tensor(here, here, eadd[:, :], ALU.add).then_inc(M_y.sem, 1)

            def final_rows(s, j, m):
                L_og.done(dve, s)
                p = part_of(s)
                V.tensor_tensor(res[j][0:p, :], x2[m][0:p, :], res[j][0:p, :], ALU.add).then_inc(L_y.sem, 1)

            def finals(h, k, j, steps, before):
                s = h * 2 - 4 + j
                if (steps or before) and not (isinstance(s, int) and s < 0):
                    final_rows(s, j, (2 * k + j) % 4)
                if not steps and before and j:
                    final_rows(NS, 0, NS % 4)

            def half2(it, k, steps, before):
                h = it * 2 + k
                if in_range(h - 2):
                    edge_scan2(h - 2, it - 1, k)
                finals(h, k, 0, steps, before)
                if steps:
                    dense_x2(h * 2, h, 0, 2 * k)
                if in_range(h):
                    edge_x2(h, it, k)
                finals(h, k, 1, steps, before)
                if steps == 2:
                    dense_x2(h * 2 + 1, h, 1, 2 * k + 1)
                for j in range(steps):
                    s = h * 2 + j
                    p = part_of(s)
                    sum_squares(stat[0:p, 1, j * R:j * R + R], sq[j][0:p, :], L_sq, s, L_ss)
                    if j == 0 and in_range(h):
                        sum_squares(stat[0:EP, 1, 2 * R:], esq[:, :], M_sq, h, M_ss)
                if in_range(h):
                    if not steps:
                        sum_squares(stat[0:EP, 1, 2 * R:], esq[:, :], M_sq, h, M_ss)
                    invert(h, steps, L_ss, M_ss, L_inv)
                for j in range(steps):
                    p = part_of(h * 2 + j)
                    t_ = rows(xc[2 * k + j][0:p, :])
                    relu_scale(t_, t_, stat[0:p, 3, j * R:j * R + R], L_h)
                if in_range(h):
                    edge_h2(h, k)
                for j in range(steps):
                    s = h * 2 + j
                    p = part_of(s)
                    L_h.done(dve, s)
                    m = 2 * k + j
                    V.tensor_tensor(x2[m][0:p, :], x2[m][0:p, :], xc[m][0:p, :], ALU.add).then_inc(L_yy.sem, 1)
                if in_range(h - 2):
                    edge_final(h - 2)

            halves(dve.Fori, half2)

        @block.scalar
        def _(act):
            A = nc.scalar

            def blocks(a, p):
                return a if p == P else a.rearrange("f (k n) -> f k n", n=P)[:, :, 0:p]

            def square(s, j, m, ready, summed, st):
                ready.done(act, s)
                summed.done(act, s - 2)
                p = part_of(s)
                A.activation(sq[j][0:p, :], xc[m][0:p, :], ACT.Square).then_inc(st.sem, 1)

            def edge_square(g, tile, ready, summed, st):
                ready.done(act, g)
                summed.done(act, g - 1)
                A.activation(esq[:, :], tile, ACT.Square).then_inc(st.sem, 1)

            def copy_hT(u, bank, ready, read, st):
                s, b, p = u.s, u.b, part_of(u.s)
                ready.part(act, s, b + 1)
                read.part(act, s - 1, b + 1)
                A.activation(blocks(hT[:, b * 512:b * 512 + 512], p), blocks(bank[:, :], p), ACT.Copy)\
                 .then_inc(st.sem, 1)

            def relu_r(u):
                s, b, p = u.s, u.b, part_of(u.s)
                S_r.part(act, s, b + 1)
                if b == 0:
                    S_gram.done(act, s - 2)
                    S_st.done(act, u.turn - 1, u.j)
                A.activation(res[u.j][0:p, b * 512:b * 512 + 512], bank_r[b][0:p, :], ACT.Relu)\
                 .then_inc(S_relu.sem, 1)

            def slot1(h, k, n, before):
                u = unit(h, k, n - 1)
                if in_work(u, n - 1, before):
                    relu_r(u)
                u = unit(h, k, n)
                if n < 2 * before:
                    copy_hT(u, bank_t[u.b], S_t, S_r, S_ht)

            def edge_exp(g):
                S_eb.done(act, g)
                S_et.done(act, g - 1)
                A.activation(weighted[:, :, D], score[:, :], ACT.Exp, bias=shift[0:EP, :])\
                 .then_inc(S_exp.sem, 1)

            def copy_hdT(g):
                S_et.done(act, g)
                S_agg.done(act, g - 1)
                A.activation(hdT[:, :], bank_d[0:D, 0:EG], ACT.Copy).then_inc(S_hd.sem, 1)

            def relu_dst(g):
                S_agg.done(act, g)
                S_ee.done(act, g - 1)
                A.activation(rdst[:, :], bank_d[0:EP, 0:EJ * D], ACT.Relu).then_inc(S_rd.sem, 1)

            def half1(it, k, steps, before):
                h = it * 2 + k
                if in_range(h - 1):
                    edge_exp(h - 1)
                if steps:
                    square(h * 2, 0, 2 * k, S_center, S_ss, S_sq)
                if in_range(h - 2):
                    relu_dst(h - 2)
                slot1(h, k, 0, before)
                if steps == 2:
                    square(h * 2 + 1, 1, 2 * k + 1, S_center, S_ss, S_sq)
                if in_range(h):
                    edge_square(h, ec[k][:, :], S_ea, S_ess, S_esq)
                slot1(h, k, 1, before)
                if in_range(h - 1):
                    copy_hdT(h - 1)
                slot1(h, k, 2, before)
                slot1(h, k, 3, before)

            act.wait_ge(s_v, 1)
            halves(act.Fori, half1)

            act.wait_ge(s_w, 16 * 23)

            def gelu_c(u):
                s, b, p = u.s, u.b, part_of(u.s)
                L_c.part(act, s, b + 1)
                L_o.part(act, s - 1, b + 1)
                for i in range(2):
                    ins = A.activation(blocks(cT[b][:, i, :], p), blocks(bank_c[b][i][0:H2, :], p), ACT.Gelu,
                                       bias=bc1[:, :])
                ins.then_inc(L_cg.sem, 1)

            def gelu_out(u):
                s, b, p = u.s, u.b, part_of(u.s)
                L_o.part(act, s, b + 1)
                if b == 0:
                    L_st.done(act, u.turn - 1, u.j)
                A.activation(res[u.j][0:p, b * 512:b * 512 + 512], bank_o[0:p, :], ACT.Gelu)\
                 .then_inc(L_og.sem, 1)

            def slot2(h, k, n, before):
                for back, do in ((1, gelu_c), (2, gelu_out)):
                    u = unit(h, k, n - back)
                    if in_work(u, n - back, before):
                        do(u)
                if n < 2 * before:
                    copy_hT(unit(h, k, n), bank_h, L_t, L_c, L_ht)

            def edge_copies(g, q):
                M_t.part(act, g, 1)
                M_m1.done(act, g - 1)
                A.activation(restT[:, :], bank_y[0:D + DE, 0:EG], ACT.Copy).then_inc(M_tc.sem, 1)
                M_t.part(act, g, 2)
                M_c.done(act, g - 2)
                A.activation(pairT[q][0:D, :], bank_x[0:D, 0:EG], ACT.Copy).then_inc(M_tc.sem, 1)

            def edge_gelu1(g):
                M_m1.done(act, g)
                M_m2.done(act, g - 1)
                A.activation(m1T[:, :], bank_y[0:H1, 0:EG], ACT.Gelu, bias=bm1[:, :]).then_inc(M_g1.sem, 1)

            def edge_gelu2(g):
                M_m2.done(act, g)
                M_scan.done(act, g - 1)
                A.activation(m2T[D:P, :], bank_x[D:P, 0:EG], ACT.Gelu, bias=bm2[D:P, :]).then_inc(M_g2.sem, 1)

            def edge_gelu_c(g, drain):
                M_c.done(act, g)
                M_o.done(act, g - 1)
                A.activation(ecT[:, :], (bank_h if drain else bank_y)[0:H2, 0:EG], ACT.Gelu, bias=bc1[:, :]).then_inc(M_cg.sem, 1)

            def edge_gelu_out(g, drain):
                M_o.done(act, g)
                M_y.done(act, g - 1)
                A.activation(eadd[:, :], (bank_o if drain else bank_x)[0:EP, 0:EJ * D], ACT.Gelu).then_inc(M_og.sem, 1)

            def half2(it, k, steps, before):
                h = it * 2 + k
                drain = not steps and not before
                if drain and in_range(h - 1):
                    edge_copies(h - 1, 1 - k)
                slot2(h, k, 0, before)
                if in_range(h - 2):
                    edge_gelu_c(h - 2, drain)
                if drain and in_range(h):
                    edge_square(h, ec[0][:, :], M_a, M_ss, M_sq)
                if drain and in_range(h - 1):
                    edge_gelu1(h - 1)
                if steps:
                    square(h * 2, 0, 2 * k, L_f, L_ss, L_sq)
                slot2(h, k, 1, before)
                if in_range(h - 2):
                    edge_gelu_out(h - 2, drain)
                if not drain and in_range(h):
                    edge_square(h, ec[0][:, :], M_a, M_ss, M_sq)
                slot2(h, k, 2, before)
                if not drain and in_range(h - 1):
                    edge_copies(h - 1, 1 - k)
                if steps == 2:
                    square(h * 2 + 1, 1, 2 * k + 1, L_f, L_ss, L_sq)
                if not drain and in_range(h - 1):
                    edge_gelu1(h - 1)
                slot2(h, k, 3, before)
                if in_range(h - 1):
                    edge_gelu2(h - 1)

            halves(act.Fori, half2)

        @block.tensor
        def _(pe):
            T = nc.tensor
            pe.wait_ge(s_v, 15)
            pe.wait_ge(s_c, 2)
            pe.wait_ge(s_w, 16 * 23)
            b_res = bias16[:, 0, :, :].rearrange("p r d -> p (r d)")
            b_out = bias16[:, 1, :, :].rearrange("p r d -> p (r d)")

            def zero_sums(start, stop):
                return T.matmul(bank_sum[:, :], wm2[:, 0:1].broadcast_to([H1, P]),
                                ones[0:H1, 0:1].broadcast_to([H1, 512]), start=start, stop=stop)

            zero_sums(True, False).then_inc(s_zero, 1)

            def transpose_h(u, bank, ready, st):
                p = part_of(u.s)
                ready.done(pe, u.s)
                for i in range(4):
                    c = (4 * u.b + i) * P
                    ins = T.transpose(bank[:, i * P:i * P + p], xc[u.m][0:p, c:c + P], ident[0:p, 0:p])
                ins.then_inc(st.sem, 1)

            def add_sums(u):
                p = part_of(u.s)
                S_relu.part(pe, u.s, u.b + 1)
                for i in range(4 * u.b, 4 * u.b + 4):
                    r_ = res[u.j][0:p, i * P:i * P + P]
                    T.matmul(bank_sum[:, 0:P], r_, r_, start=False, stop=False)
                    ins = T.matmul(bank_sum[:, P:P + 1], r_, ones[0:p, 0:1], start=False, stop=False)
                ins.then_inc(S_gram.sem, 1)

            def r_product(u):
                s, b, p = u.s, u.b, part_of(u.s)
                S_ht.part(pe, s, b + 1)
                S_relu.part(pe, s - 1, b + 1)
                for i in range(4):
                    c = (4 * b + i) * P
                    T.matmul(bank_r[b][0:p, i * P:i * P + P], hT[:, c:c + p], wres2[:, :],
                             start=(i == 0), stop=False)
                T.matmul(bank_r[b][0:p, :], ones16[:, 0:p], b_res, start=False, stop=True)\
                 .then_inc(S_r.sem, 1)

            def slot1(h, k, n, before):
                for back, do in ((2, add_sums), (1, r_product)):
                    u = unit(h, k, n - back)
                    if in_work(u, n - back, before):
                        do(u)
                if n < 2 * before:
                    u = unit(h, k, n)
                    S_ht.part(pe, u.s - 1, u.b + 1)
                    transpose_h(u, bank_t[u.b], S_h, S_t)

            def edge_transposes(g, k):
                S_ew.done(pe, g)
                S_scan.done(pe, g - 1)
                S_rd.done(pe, g - 1)
                for j in range(EJ):
                    T.transpose(bank_w[0:D + 1, j:EG:EJ], weighted[:, j, :], ident[0:EP, 0:EP])
                    ins = T.transpose(bank_d[0:D, j:EG:EJ], ec[k][:, (EJ + j) * D:(EJ + j + 1) * D],
                                      ident[0:EP, 0:EP])
                ins.then_inc(S_et.sem, 1)

            def edge_products(g, q):
                S_scan.done(pe, g)
                S_hd.done(pe, g)
                S_ee.done(pe, g - 1)
                for j in range(EJ):
                    ins = T.matmul(bank_a[0:EP, j * (D + 1):(j + 1) * (D + 1)], sums[q][:, j:EG:EJ],
                                   wconv[:, :], start=(j == 0), stop=(j == EJ - 1))
                ins.then_inc(S_agg.sem, 1)
                for j in range(EJ):
                    T.matmul(bank_d[0:EP, j * D:(j + 1) * D], hdT[:, j:EG:EJ], wres2[0:D, 0:D],
                             start=(j == 0), stop=False)
                T.matmul(bank_d[0:EP, 0:EJ * D], ones16[:, 0:EP], b_res[:, 0:EJ * D], start=False, stop=True)\
                 .then_inc(S_agg.sem, 1)

            def edge_stats(g):
                S_ee.done(pe, g)
                for j in range(EJ):
                    c = last[:, g * EJ + j:g * EJ + j + 1] if isinstance(g, int) else \
                        last[:, bass.ds(g * EJ + j, 1)]
                    ins = T.matmul(bank_sum[:, P + 1:P + 2], diff[:, j, :], c, start=False, stop=False)
                ins.then_inc(S_es.sem, 1)

            def half1(it, k, steps, before):
                h = it * 2 + k
                if in_range(h - 2):
                    edge_products(h - 2, k)
                slot1(h, k, 0, before)
                slot1(h, k, 1, before)
                if in_range(h - 1):
                    edge_transposes(h - 1, 1 - k)
                slot1(h, k, 2, before)
                slot1(h, k, 3, before)
                if in_range(h - 2):
                    edge_stats(h - 2)

            pe.wait_ge(s_zero, 1)
            halves(pe.Fori, half1)
            zero_sums(False, True).then_inc(S_es.sem, 1)

            pe.wait_ge(s_bnd, BN_PARTS)
            T.matmul(bank_r[0][:, 0:P], ones[:, :], bnz[:, 0, :, :].rearrange("p a d -> p (a d)"),
                     start=True, stop=False)
            T.matmul(bank_r[0][:, 0:P], ones[:, :], bnz[:, 1, :, :].rearrange("p a d -> p (a d)"),
                     start=False, stop=True).then_inc(s_bnp, 1)
            pe.wait_ge(s_bnd, BN_PARTS + 1)

            def c_product(u):
                s, b, p = u.s, u.b, part_of(u.s)
                L_ht.part(pe, s, b + 1)
                L_cg.part(pe, s - 1, b + 1)
                for i in range(2):
                    o = bank_c[b][i][0:H2, :]
                    a = hT[i * D:i * D + D, b * 512:b * 512 + 512]
                    if p != P:
                        o = o.rearrange("f (k n) -> f k n", n=P)[:, :, 0:p]
                        a = a.rearrange("f (k n) -> f k n", n=P)[:, :, 0:p]
                    ins = T.matmul(o, wc1_node[i * D:i * D + D, :], a, start=True, stop=True)
                ins.then_inc(L_c.sem, 1)

            def out_product(u):
                s, b, p = u.s, u.b, part_of(u.s)
                L_cg.part(pe, s, b + 1)
                if b:
                    L_og.part(pe, s, 1)
                else:
                    L_og.done(pe, s - 1)
                for i in range(8):
                    T.matmul(bank_o[0:p, i * D:i * D + D], cT[b][:, i % 2, (i // 2) * P:(i // 2) * P + p],
                             wc2[:, :], start=(i == 0), stop=False)
                T.matmul(bank_o[0:p, :], ones16[:, 0:p], b_out, start=False, stop=True).then_inc(L_o.sem, 1)

            def slot2(h, k, n, before):
                for back, do in ((1, c_product), (2, out_product)):
                    u = unit(h, k, n - back)
                    if in_work(u, n - back, before):
                        do(u)
                if n < 2 * before:
                    u = unit(h, k, n)
                    if u.b:
                        L_ht.part(pe, u.s, 1)
                    else:
                        L_ht.done(pe, u.s - 1)
                    transpose_h(u, bank_h, L_h, L_t)

            def edge_transposes2(g, q, read_y, read_x):
                M_b.part(pe, g, 2)
                read_y.done(pe, g - 1)
                read_x.done(pe, g - 1)
                for j in range(EJ):
                    ins = T.transpose(bank_y[0:D + DE, j:EG:EJ], hsrc[q][:, j, :], ident[0:EP, 0:EP])
                ins.then_inc(M_t.sem, 1)
                for j in range(EJ):
                    ins = T.transpose(bank_x[0:D, j:EG:EJ], hdst[:, j * D:j * D + D], ident[0:EP, 0:EP])
                ins.then_inc(M_t.sem, 1)

            def edge_message1(g, q):
                M_tc.done(pe, g)
                T.matmul(bank_y[0:H1, 0:EG], wm1_rest[:, :], restT[:, :], start=True, stop=False)
                T.matmul(bank_y[0:H1, 0:EG], wm1_dst[:, :], pairT[q][0:D, :], start=False, stop=True)\
                 .then_inc(M_m1.sem, 1)

            def edge_message2(g):
                M_g1.done(pe, g)
                T.matmul(bank_x[:, 0:EG], wm2[:, :], m1T[:, :], start=True, stop=True).then_inc(M_m2.sem, 1)

            def edge_c(g, q, drain):
                M_scan.done(pe, g)
                if drain:
                    M_cg.done(pe, g - 1)
                T.matmul((bank_h if drain else bank_y)[0:H2, 0:EG], wc1[:, :], pairT[q][:, :], start=True, stop=True)\
                 .then_inc(M_c.sem, 1)

            def edge_out(g, drain):
                bank = bank_o if drain else bank_x
                if drain:
                    M_og.done(pe, g - 1)
                else:
                    M_g2.done(pe, g)
                M_cg.done(pe, g)
                for j in range(EJ):
                    T.matmul(bank[0:EP, j * D:(j + 1) * D], ecT[:, j:EG:EJ], wc2[:, :],
                             start=(j == 0), stop=False)
                T.matmul(bank[0:EP, 0:EJ * D], ones16[:, 0:EP], b_out[:, 0:EJ * D], start=False, stop=True)\
                 .then_inc(M_o.sem, 1)

            def half2(it, k, steps, before):
                h = it * 2 + k
                drain = not steps and not before
                if drain and in_range(h - 1):
                    edge_transposes2(h - 1, 1 - k, M_g1, M_g2)
                slot2(h, k, 0, before)
                if in_range(h - 2):
                    edge_c(h - 2, k, drain)
                if drain and in_range(h - 1):
                    edge_message1(h - 1, 1 - k)
                slot2(h, k, 1, before)
                if in_range(h - 2):
                    edge_out(h - 2, drain)
                slot2(h, k, 2, before)
                if not drain and in_range(h - 1):
                    edge_transposes2(h - 1, 1 - k, M_cg, M_og)
                    edge_message1(h - 1, 1 - k)
                slot2(h, k, 3, before)
                if in_range(h - 1):
                    edge_message2(h - 1)

            halves(pe.Fori, half2)


_INS = ["x", "src", "dst", "edge_attr_32", "L0_gnn_W_conv", "L0_gnn_b_conv", "L0_gnn_W_res", "L0_gnn_b_res",
        "L0_gnn_gamma", "L0_gnn_beta", "L1_gnn_W_m1", "L1_gnn_b_m1", "L1_gnn_W_m2", "L1_gnn_b_m2",
        "L1_gnn_W_c1", "L1_gnn_b_c1", "L1_gnn_W_c2", "L1_gnn_b_c2"]


def kernel(**inputs):
    import numpy as np
    import concourse.bacc as bacc
    from concourse.bass_utils import run_bass_kernel_spmd as run

    nc = bacc.Bacc("TRN2", target_bir_lowering=False, num_devices=1)
    arrays, aps = {}, {}
    for name in _INS:
        a = np.ascontiguousarray(inputs[name])
        arrays[f"in_{name}"] = a
        aps[name] = nc.dram_tensor(f"in_{name}", a.shape, mybir.dt.from_np(a.dtype), kind="ExternalInput").ap()
    out = nc.dram_tensor("out_0", arrays["in_x"].shape, F32, kind="ExternalOutput").ap()
    program(nc, aps, out)
    r = run(nc, [arrays], core_ids=[0])
    return r.results[0]["out_0"]
```

```python
from contextlib import ExitStack

import concourse.bass as bass
from concourse import mybir

F32 = mybir.dt.float32
BF16 = mybir.dt.bfloat16
I32 = mybir.dt.int32
ALU = mybir.AluOpType
ACT = mybir.ActivationFunctionType
AX = mybir.AxisListType.X

P = 128
D = 64
DE = 32
EP = 125
EJ = 4
EG = EP * EJ
R = 16
RD = R * D
PAIRS = R // 2
STEP = P * R
LN_EPS = 1e-5
BN_EPS = 1e-5
SHIFT = 32.0
BEYOND = 1048576
MAGIC = float(0x5F3759DF)
NEWTON = 10
BN_PARTS = 8


class Stage:

    def __init__(self, sem, incs=1):
        self.sem, self.incs = sem, incs

    def after(self, step, k=None):
        return step * self.incs + (self.incs if k is None else k)

    def done(self, eng, step):
        if isinstance(step, int) and step < 0:
            return
        eng.wait_ge(self.sem, step * self.incs + self.incs)

    def part(self, eng, step, k):
        if isinstance(step, int) and step < 0:
            return
        eng.wait_ge(self.sem, step * self.incs + k)


class Unit:

    def __init__(self, s, b, j, m, turn):
        self.s, self.b = s, b
        self.j, self.m = j, m
        self.turn = turn


class Slots:

    def __init__(self, sems, incs=16):
        self.sems, self.incs = sems, incs

    def after(self, turn):
        return turn * self.incs + self.incs

    def done(self, eng, turn, q):
        if isinstance(turn, int) and turn < 0:
            return
        eng.wait_ge(self.sems[q], turn * self.incs + self.incs)


def program(nc, t, out):
    x, src, dst, ea = t["x"], t["src"], t["dst"], t["edge_attr_32"]
    N = x.shape[0]
    E = src.shape[0]
    G = E // EG
    NS = N // STEP
    PT = (N - NS * STEP) // R
    HD = NS // 2
    BODY = HD // 2
    GB = G // 2
    assert G * EG == E and NS % 4 == 0 and PT * R + NS * STEP == N and PT <= P and G % 2 == 0
    assert N < 1 << 20 and G == 2 * HD + 2 and G % 4 == 2
    H1 = t["L1_gnn_W_m1"].shape[1]
    H2 = t["L1_gnn_W_c1"].shape[1]

    with ExitStack() as ctx:
        def sb(name, shape, dt=F32):
            return ctx.enter_context(nc.sbuf_tensor(name, shape, dt))

        def pb(name):
            return ctx.enter_context(nc.psum_tensor(name, [P, 512], F32))

        def sem(name):
            return ctx.enter_context(nc.semaphore(name))

        def stage(name, incs=1):
            return Stage(sem(name), incs)

        def slots(name, incs=16, n=2):
            return Slots([sem(f"{name}{q}") for q in range(n)], incs)

        table = nc.dram_tensor("layer0_rows", (N, D), F32).ap()
        layer0_edge_rows = nc.dram_tensor("layer0_edge_rows", (G, EP, 2 * EJ * D), F32).ap()
        edge_rows = nc.dram_tensor("edge_rows", (G, EP, 2 * EJ * D), F32).ap()
        dst_pad = nc.dram_tensor("dst_pad", (E + 2,), I32).ap()
        same_row = nc.dram_tensor("same_row", (E,), F32).ap()
        put_row = nc.dram_tensor("put_row", (E,), I32).ap()

        ident = sb("ident", [P, P])
        ones = sb("ones", [P, P])
        ones16 = sb("ones16", [D + 1, P], BF16)
        shift = sb("shift", [P, 1])
        wres2 = sb("wres2", [P, P])
        wconv = sb("wconv", [D + 1, D + 1])
        bias_in = sb("bias_in", [D + 1, 2, D])
        bias_rest = sb("bias_rest", [D + 1, 2, 2, D])
        bias_part = sb("bias_part", [D + 1, 3, 2, D], BF16)
        bias16 = sb("bias16", [D + 1, 2, 8, D], BF16)
        wc1_node = sb("wc1_node", [P, H2])
        wc1 = sb("wc1", [P, H2])
        wc2 = sb("wc2", [H2, D])
        wm1_dst = sb("wm1_dst", [D, H1])
        wm1_rest = sb("wm1_rest", [D + DE, H1])
        wm2 = sb("wm2", [H1, P])
        bm1 = sb("bm1", [H1, 1])
        bm2 = sb("bm2", [P, 1])
        bc1 = sb("bc1", [H2, 1])
        bn_in = sb("bn_in", [P, 2, D])
        bn = sb("bn", [P, 2, D])

        dst_idx = sb("dst_idx", [EP, G * EJ], I32)
        next_idx = sb("next_idx", [EP, G * EJ], I32)
        put_idx = sb("put_idx", [EP, G * EJ], I32)
        get_idx = [sb(f"get_idx{q}", [EP, 2 * EJ], I32) for q in range(4)]
        put_now = [sb(f"put_now{i}", [EP, EJ], I32) for i in range(4)]
        put_rows = [sb(f"put_rows{i}", [EP, EJ * D]) for i in range(4)]
        last = sb("last", [EP, G * EJ])
        flat = sb("flat", [EP, 2, E // EP], I32)
        same_flat = sb("same_flat", [EP, E // EP])
        end_mark = sb("end_mark", [1, 2], I32)

        xin = [sb(f"xin{q}", [P, RD]) for q in range(2)]
        rin = [sb(f"rin{q}", [P, RD]) for q in range(2)]
        xc = [sb(f"xc{q}", [P, RD]) for q in range(4)]
        x2 = [sb(f"x2_{q}", [P, RD]) for q in range(4)]
        sq = [sb(f"sq{q}", [P, RD]) for q in range(2)]
        hT = sb("hT", [P, RD])
        res = [sb(f"res{q}", [P, PAIRS, P + 1]) for q in range(2)]
        cT = [sb(f"cT{b}", [H2, 2, 512]) for b in range(2)]
        stat = sb("stat", [P, 5, 2 * R + 2 * EJ])

        ring = [sb(f"ring{q}", [EP, 2 * EJ * D]) for q in range(4)]
        eg = [sb(f"eg{q}", [EP, 2 * EJ * D]) for q in range(2)]
        er = [sb(f"er{q}", [EP, 2 * EJ * D]) for q in range(2)]
        ec = [sb(f"ec{q}", [EP, 2 * EJ * D]) for q in range(2)]
        ex = sb("ex", [EP, 2 * EJ * D])
        esq = sb("esq", [EP, 2 * EJ * D])
        prod = sb("prod", [EP, EJ * D])
        score = sb("score", [EP, EJ])
        weighted = sb("weighted", [EP, EJ, D + 1])
        same = [sb(f"same{q}", [P, EG]) for q in range(2)]
        sums = [sb(f"sums{q}", [D + 1, EG]) for q in range(2)]
        hdT = sb("hdT", [D, EG])
        rdst = sb("rdst", [EP, EJ * D])
        inv = sb("inv", [EP, EJ])
        diff = sb("diff", [EP, EJ, 2 * D])
        twice = sb("twice", [EP, EJ * D])
        dst_rows = sb("dst_rows", [EP, G * EJ * D])
        hsrc = [sb(f"hsrc{q}", [EP, EJ, D + DE]) for q in range(2)]
        hdst = sb("hdst", [EP, EJ * D])
        restT = sb("restT", [D + DE, EG])
        m1T = sb("m1T", [H1, EG])
        m2T = sb("m2T", [P, EG])
        pairT = [sb(f"pairT{q}", [P, EG]) for q in range(2)]
        ecT = sb("ecT", [H2, EG])
        eadd = sb("eadd", [EP, EJ * D])

        bnz = sb("bnz", [P, 2, 2, D])
        bncol = sb("bncol", [P, 4])
        bndiag = sb("bndiag", [P, P])
        bnw = sb("bnw", [P, 8, D])

        B = [pb(f"bank{i}") for i in range(8)]
        bank_t, bank_r, bank_sum = B[0:2], B[2:4], B[4]
        bank_w, bank_d, bank_a = B[5], B[6], B[7]
        bank_h, bank_c, bank_o = B[0], (B[1:3], B[3:5]), B[5]
        bank_x, bank_y = B[6], B[7]

        s_w = sem("weights_loaded")
        s_dst = sem("dst_loaded")
        s_pad = sem("dst_padded")
        s_flat = sem("dst_windows_loaded")
        s_sameput = sem("same_row_stored")
        s_puts = sem("put_row_stored")
        s_c = sem("pool_constants")
        s_v = sem("vector_setup")
        s_zero = sem("sums_bank_cleared")
        S_ix = slots("get_idx_loaded", 32, 4)
        S_get = slots("x_gathered", 16 * 2 * EJ, 4)
        S_stash = slots("x_stashed", 16, 4)
        S_eg = slots("edge_x_loaded")
        S_same = slots("same_loaded")
        S_px = slots("put_loaded", 32, 4)
        S_put = slots("layer0_rows_scattered", 16 * EJ, 4)
        S_x = slots("x_loaded")
        S_st = slots("r_stored")
        S_center = stage("centered", 2)
        S_sq = stage("squared")
        S_ss = stage("squares_summed")
        S_inv = stage("deviations_inverted", NEWTON + 1)
        S_h = stage("h_ready")
        S_t = stage("h_transposed", 2)
        S_ht = stage("hT_copied", 2)
        S_r = stage("r_product", 2)
        S_relu = stage("r_ready", 2)
        S_gram = stage("r_summed", 2)
        S_ea = stage("edge_centered", 2)
        S_esq = stage("edge_squared")
        S_ess = stage("edge_squares_summed")
        S_eb = stage("edge_scored", 3)
        S_exp = stage("edge_exp")
        S_ew = stage("edge_weighted")
        S_et = stage("edge_transposed")
        S_hd = stage("hdT_copied")
        S_scan = stage("segment_summed")
        S_agg = stage("edge_products", 2)
        S_rd = stage("r_of_dst")
        S_ee = stage("dst_row_ready", 5)
        S_es = stage("edge_stats_added")
        s_first = sem("first_group_stashed")
        s_bnp = sem("bn_summed")
        s_bnd = sem("bn_vector")
        L_ix = slots("get_idx_reloaded", 32, 4)
        L_get = slots("layer0_rows_gathered", 16 * 2 * EJ, 4)
        L_stash = slots("layer0_rows_stashed", 16, 4)
        M_ld = slots("edge_rows_loaded", 48)
        M_same = slots("same_reloaded")
        L_px = slots("final_put_loaded", 32, 4)
        L_put = slots("final_rows_scattered", 16 * EJ, 4)
        L_x = slots("rows_loaded", 32)
        L_st = slots("final_rows_stored")
        L_f = stage("x2_centered", 5)
        L_sq = stage("x2_squared")
        L_ss = stage("x2_squares_summed")
        L_inv = stage("x2_deviations_inverted", NEWTON + 1)
        L_h = stage("h2_ready")
        L_yy = stage("x2_plus_h2")
        L_t = stage("h2_transposed", 2)
        L_ht = stage("h2T_copied", 2)
        L_c = stage("c_product", 2)
        L_cg = stage("c_gelu", 2)
        L_o = stage("out_product", 2)
        L_og = stage("out_gelu", 2)
        L_y = stage("final_row_ready")
        M_a = stage("edge_x2_centered", 5)
        M_sq = stage("edge_x2_squared")
        M_ss = stage("edge_x2_squares_summed")
        M_b = stage("edge_h2_ready", 3)
        M_t = stage("edge_h2_transposed", 2)
        M_tc = stage("edge_h2T_copied", 2)
        M_m1 = stage("message1_product")
        M_g1 = stage("message1_gelu")
        M_m2 = stage("message2_product")
        M_g2 = stage("message2_gelu")
        M_scan = stage("messages_summed")
        M_c = stage("edge_c_product")
        M_cg = stage("edge_c_gelu")
        M_o = stage("edge_out_product")
        M_og = stage("edge_out_gelu")
        M_y = stage("dst_final_ready")

        main = NS * STEP

        def dense_rows(a, s, p):
            if p == P:
                v = a[0:main, :].rearrange("(s p r) d -> s p (r d)", p=P, r=R)
                return v[s, :, :] if isinstance(s, int) else v[bass.ds(s, 1), :, :].rearrange("a p n -> (a p) n")
            return a[main:N, :].rearrange("(p r) d -> p (r d)", r=R)

        def pairs(a):
            return a.rearrange("p (k n) -> p k n", n=P)

        def one(a, g):
            if isinstance(g, int):
                return a[g]
            v = a[bass.ds(g, 1)]
            return v.rearrange("a p n -> (a p) n") if len(v.shape) == 3 else v.rearrange("a n -> (a n)")

        def rows(a):
            return a.rearrange("p (r d) -> p r d", d=D)

        def per_row(a, n=D):
            return a.unsqueeze(2).broadcast_to([a.shape[0], a.shape[1], n])

        def cols(a, w):
            return a.unsqueeze(1).broadcast_to([a.shape[0], w, a.shape[1]])

        def group_cols(t2, g, w=EJ * D):
            return t2[:, bass.ds(g * w, w)] if not isinstance(g, int) else t2[:, g * w:g * w + w]

        def in_range(g):
            return not isinstance(g, int) or 0 <= g < G

        def halves(loop, half):
            for k in range(4):
                half(k // 2, k % 2, 2, 2 if k else 0)
            with loop(2, BODY) as it:
                half(it, 0, 2, 2)
                half(it, 1, 2, 2)
            half(BODY, 0, 1, 2)
            half(BODY, 1, 0, 1)
            with loop(BODY + 1, GB) as it:
                half(it, 0, 0, 0)
                half(it, 1, 0, 0)
            half(GB, 0, 0, 0)
            half(GB, 1, 0, 0)

        def unit(h, k, n):
            a = n // 2
            return Unit(s=h * 2 + (a - 2), b=n % 2, j=a % 2, m=(2 * k - 2 + a) % 4,
                                   turn=h + (a // 2 - 1))

        def in_work(u, n, before):
            if isinstance(u.s, int):
                return (0 <= u.s <= NS) and (before > 0)
            return before > 0

        def products_banks(k, dense):
            return (bank_a, bank_d) if dense else ((bank_r[0], bank_a)[k], bank_t[0])

        def part_of(s):
            return PT if isinstance(s, int) and s == NS else P

        block = ctx.enter_context(nc.Block())

        @block.sync
        def _(sp):
            def load_small(dst_ap, src_ap):
                sp.dma_start(dst_ap, src_ap).then_inc(s_w, 16)

            def edge_values(a, g):
                return one(a.rearrange("(g p j) -> g p j", p=EP, j=EJ), g)

            def load_idx(g, q, loaded):
                sp.dma_start(get_idx[q][:, 0:EJ], edge_values(src, g)).then_inc(loaded.sems[q], 16)
                sp.dma_start(get_idx[q][:, EJ:2 * EJ], edge_values(dst, g)).then_inc(loaded.sems[q], 16)

            for g in range(4):
                load_idx(g, g, S_ix)
            sp.dma_start(dst_idx[:, :].rearrange("p (g j) -> p g j", j=EJ),
                         dst.rearrange("(g p j) -> p g j", p=EP, j=EJ)).then_inc(s_dst, 16)

            def col(a):
                return a.rearrange("(n a) -> n a", a=1)

            def row(a):
                return a.rearrange("(a n) -> a n", a=1)

            sp.wait_ge(s_v, 1)
            load_small(wres2[0:D, 0:D], t["L0_gnn_W_res"])
            load_small(wres2[D:P, D:P], t["L0_gnn_W_res"])
            load_small(wconv[0:D, 0:D], t["L0_gnn_W_conv"])
            load_small(wconv[D:D + 1, 0:D], row(t["L0_gnn_b_conv"]))
            for p in (0, 32, 64):
                load_small(bias_in[p:p + 1, 0, :], row(t["L0_gnn_b_res"]))
                load_small(bias_in[p:p + 1, 1, :], row(t["L1_gnn_b_c2"]))
            load_small(wc1_node[0:D, :], t["L1_gnn_W_c1"][0:D, :])
            load_small(wc1_node[D:P, :], t["L1_gnn_W_c1"][0:D, :])
            load_small(wc1[:, :], t["L1_gnn_W_c1"])
            load_small(wc2[:, :], t["L1_gnn_W_c2"])
            load_small(wm1_dst[:, :], t["L1_gnn_W_m1"][D:2 * D, :])
            load_small(wm1_rest[0:D, :], t["L1_gnn_W_m1"][0:D, :])
            load_small(wm1_rest[D:D + DE, :], t["L1_gnn_W_m1"][2 * D:2 * D + DE, :])
            load_small(wm2[:, D:P], t["L1_gnn_W_m2"])
            load_small(bm1[:, :], col(t["L1_gnn_b_m1"]))
            load_small(bm2[D:P, :], col(t["L1_gnn_b_m2"]))
            load_small(bc1[:, :], col(t["L1_gnn_b_c1"]))
            load_small(bn_in[:, 0, :], row(t["L0_gnn_gamma"]).broadcast_to([P, D]))
            load_small(bn_in[:, 1, :], row(t["L0_gnn_beta"]).broadcast_to([P, D]))

            sp.dma_start(dst_pad[1:E + 1], dst).then_inc(s_pad, 16)
            sp.dma_start(dst_pad[0:1].rearrange("(a n) -> a n", a=1), end_mark[:, 0:1]).then_inc(s_pad, 16)
            sp.dma_start(dst_pad[E + 1:E + 2].rearrange("(a n) -> a n", a=1),
                         end_mark[:, 1:2]).then_inc(s_pad, 16)
            sp.wait_ge(s_pad, 48)
            for k in range(2):
                sp.dma_start(flat[:, k, :], dst_pad[k:E + k].rearrange("(p c) -> p c", p=EP))\
                  .then_inc(s_flat, 16)
            sp.dma_start(next_idx[:, :].rearrange("p (g j) -> p g j", j=EJ),
                         dst_pad[2:E + 2].rearrange("(g p j) -> p g j", p=EP, j=EJ)).then_inc(s_flat, 16)
            sp.wait_ge(s_v, 3)
            sp.dma_start(same_row.rearrange("(p c) -> p c", p=EP), same_flat[:, :]).then_inc(s_sameput, 16)
            sp.wait_ge(s_v, 4)
            sp.dma_start(put_row.rearrange("(g p j) -> p g j", p=EP, j=EJ),
                         put_idx[:, :].rearrange("p (g j) -> p g j", j=EJ)).then_inc(s_puts, 16)
            sp.wait_ge(s_sameput, 16)
            sp.wait_ge(s_puts, 16)

            def stash(it, i, got, rows_dram, stashed, loaded, more):
                sp.wait_ge(got.sems[i], got.after(it))
                sp.dma_start(one(rows_dram, it * 4 + i), ring[i][:, :]).then_inc(stashed.sems[i], 16)
                if more:
                    load_idx(it * 4 + (i + 4), i, loaded)

            def stashed_before(h, it, k, stashed):
                if not isinstance(h, int):
                    if it is not None:
                        stashed.done(sp, it - (1 - k), 0)
                        for i in range(1, 4):
                            stashed.done(sp, it - 1, i)
                elif h < 4:
                    stashed.done(sp, (h + 1) // 4, (h + 1) % 4)
                elif h == HD + 1:
                    for i in range(4):
                        stashed.done(sp, (G - 1 - i) // 4, i)

            def load_same(g, q, p0, p1, scanned, loaded):
                scanned.done(sp, g - 2)
                sp.dma_start(same[q][p0:p1, :], one(same_row.rearrange("(g n) -> g n", n=EG), g)
                             .unsqueeze(0).broadcast_to([p1 - p0, EG])).then_inc(loaded.sems[q], 16)

            def load_put(g, turn, i, ready, loaded, put):
                sp.wait_ge(ready.sem, ready.after(g))
                put.done(sp, turn - 1, i)
                sp.dma_start(put_now[i][:, :], edge_values(put_row, g)).then_inc(loaded.sems[i], 16)
                sp.dma_start(put_rows[i][:, :], group_cols(dst_rows, g)).then_inc(loaded.sems[i], 16)

            def load_puts(it, k, ready, loaded, put):
                for j in range(2):
                    i = (2 * k + 2 + j) % 4
                    load_put(it * 4 + (2 * k + j - 2 * HD - 2), it - (BODY + 1) + k, i, ready, loaded, put)

            def sync_halves(dense, edge, gets, puts):
                def half(it, k, steps, before):
                    h = it * 2 + k
                    dense(h, steps, before)
                    if steps:
                        for j in range(2):
                            if not isinstance(h, int) or h < HD or 2 * h + j < G:
                                stash(it, 2 * k + j, *gets, not isinstance(h, int) or 2 * h + j + 4 < G)
                    edge(h, it, k, steps > 0)
                    if not steps:
                        load_puts(it, k, *puts)

                for k in range(4):
                    half(k // 2, k % 2, 2, 2 if k else 0)
                with sp.Fori(2, BODY - 1) as it:
                    half(it, 0, 2, 2)
                    half(it, 1, 2, 2)
                half(BODY - 1, 0, 2, 2)
                half(BODY - 1, 1, 2, 2)
                half(BODY, 0, 1, 2)
                half(BODY, 1, 0, 1)
                with sp.Fori(BODY + 1, GB - 1) as it:
                    half(it, 0, 0, 0)
                    half(it, 1, 0, 0)
                half(GB - 1, 0, 0, 0)
                half(GB - 1, 1, 0, 0)

            def load_x(s, turn, j):
                S_center.done(sp, s - 2)
                p = part_of(s)
                sp.dma_start(xin[j][0:p, :], dense_rows(x, s, p)).then_inc(S_x.sems[j], 16)

            def store_r(s, j):
                sp.wait_ge(S_relu.sem, S_relu.after(s))
                p = part_of(s)
                sp.dma_start(pairs(dense_rows(table, s, p)), res[j][0:p, :, 0:P]).then_inc(S_st.sems[j], 16)

            def dense1(h, steps, before):
                if steps == 2:
                    for j in range(2):
                        if not isinstance(h, int) or 2 * h + 2 + j <= NS:
                            load_x(h * 2 + (2 + j), h + 1, j)
                for s, j in ((h * 2 - 3, 1), (h * 2 - 2, 0)):
                    if (steps or before) and not (isinstance(s, int) and s < 0):
                        store_r(s, j)

            def edge1(h, it, k, stashing):
                load_same(h, k, 0, D + 1, S_scan, S_same)
                if in_range(h + 1):
                    stashed_before(h, it if stashing else None, k, S_stash)
                    S_ea.done(sp, h - 1)
                    sp.dma_start(eg[1 - k][:, :], one(edge_rows, h + 1)).then_inc(S_eg.sems[1 - k], 16)

            load_x(0, 0, 0)
            load_x(1, 0, 1)
            sp.wait_ge(S_get.sems[0], S_get.after(0))
            sp.dma_start(edge_rows[0], ring[0][:, :]).then_inc(s_first, 16)
            sp.wait_ge(s_first, 16)
            sp.dma_start(eg[0][:, :], edge_rows[0]).then_inc(S_eg.sems[0], 16)
            sync_halves(dense1, edge1, (S_get, edge_rows, S_stash, S_ix), (S_ee, S_px, S_put))

            for q in range(2):
                sp.wait_ge(S_st.sems[q], S_st.after((NS - q) // 2))
            for i in range(4):
                sp.wait_ge(S_put.sems[i], S_put.after((G - 1 - i) // 4))
                load_idx(i, i, L_ix)

            def load_rows(s, turn, j):
                L_f.done(sp, s - 2)
                p = part_of(s)
                sp.dma_start(xin[j][0:p, :], dense_rows(x, s, p)).then_inc(L_x.sems[j], 16)
                sp.dma_start(rin[j][0:p, :], dense_rows(table, s, p)).then_inc(L_x.sems[j], 16)

            def store_final(s, j):
                sp.wait_ge(L_y.sem, L_y.after(s))
                p = part_of(s)
                sp.dma_start(pairs(dense_rows(out, s, p)), res[j][0:p, :, 0:P]).then_inc(L_st.sems[j], 16)

            def dense2(h, steps, before):
                for j in range(2):
                    s = h * 2 - 4 + j
                    if (steps or before) and not (isinstance(s, int) and s < 0):
                        store_final(s, j)
                if steps == 0 and before:
                    store_final(NS, 0)
                if steps == 2:
                    for j in range(2):
                        if not isinstance(h, int) or 2 * h + 2 + j <= NS:
                            load_rows(h * 2 + (2 + j), h + 1, j)

            def load_edges(g, q):
                M_a.done(sp, g - 2)
                sp.dma_start(eg[q][:, :], one(edge_rows, g)).then_inc(M_ld.sems[q], 16)
                sp.dma_start(er[q][:, :], one(layer0_edge_rows, g)).then_inc(M_ld.sems[q], 16)
                M_t.done(sp, g - 2)
                sp.dma_start(hsrc[q][:, :, D:D + DE],
                             one(ea.rearrange("(g p j) d -> g p (j d)", p=EP, j=EJ), g)
                             .rearrange("p (j d) -> p j d", d=DE)).then_inc(M_ld.sems[q], 16)

            def edge2(h, it, k, stashing):
                load_same(h, k, D, P, M_scan, M_same)
                if in_range(h + 1):
                    stashed_before(h, it if stashing else None, k, L_stash)
                    load_edges(h + 1, 1 - k)

            load_rows(0, 0, 0)
            load_rows(1, 0, 1)
            sp.wait_ge(L_get.sems[0], L_get.after(0))
            sp.dma_start(layer0_edge_rows[0], ring[0][:, :]).then_inc(s_first, 16)
            sp.wait_ge(s_first, 32)
            load_edges(0, 0)
            sync_halves(dense2, edge2, (L_get, layer0_edge_rows, L_stash, L_ix), (M_y, L_px, L_put))
            for q in range(2):
                sp.wait_ge(L_st.sems[q], L_st.after((NS - q) // 2))
            for i in range(4):
                sp.wait_ge(L_put.sems[i], L_put.after((G - 1 - i) // 4))

        @block.gpsimd
        def _(pool):
            nc.gpsimd.memset(ident[:, :], 0.0).then_inc(s_c, 1)
            nc.gpsimd.memset(ones[:, :], 1.0)
            nc.gpsimd.memset(ones16[:, :], 1.0)
            pool.wait_ge(s_c, 1)
            nc.gpsimd.affine_select(out=ident[:, :], in_=ident[:, :], compare_op=ALU.not_equal, fill=1.0,
                                    base=0, pattern=[[-1, P]], channel_multiplier=1).then_inc(s_c, 1)
            limit = pool.to_reg(N - 1)
            nodes = pool.to_reg(N)

            def waits_end():
                pool.reg_add(limit, nodes, -1)

            def gather(turn, i, source, loaded, stashed, got):
                pool.wait_ge(loaded.sems[i], loaded.after(turn))
                stashed.done(pool, turn - 1, i)
                waits_end()
                for j in range(2 * EJ):
                    nc.gpsimd.indirect_dma_start(ring[i][:, j * D:j * D + D], None, source[:, :],
                                                 bass.IndirectOffsetOnAxis(ap=get_idx[i][:, j:j + 1], axis=0),
                                                 bounds_check=limit, oob_is_err=False)\
                      .then_inc(got.sems[i], 16)

            def scatter(turn, i, target, loaded, put):
                pool.wait_ge(loaded.sems[i], loaded.after(turn))
                waits_end()
                for j in range(EJ):
                    nc.gpsimd.indirect_dma_start(target[:, :],
                                                 bass.IndirectOffsetOnAxis(ap=put_now[i][:, j:j + 1], axis=0),
                                                 put_rows[i][:, j * D:j * D + D], None,
                                                 bounds_check=limit, oob_is_err=False).then_inc(put.sems[i], 16)

            def groups(do, *args):
                for i in range(4):
                    do(0, i, *args)
                with pool.Fori(1, G // 4) as turn:
                    for i in range(4):
                        do(turn, i, *args)
                for i in range(G % 4):
                    do(G // 4, i, *args)

            groups(gather, x, S_ix, S_stash, S_get)
            for q in range(2):
                pool.wait_ge(S_st.sems[q], S_st.after((NS - q) // 2))
            groups(scatter, table, S_px, S_put)
            for i in range(4):
                pool.wait_ge(S_put.sems[i], S_put.after((G - 1 - i) // 4))

            def half2(it, k, steps, before):
                h = it * 2 + k
                if not steps:
                    return
                for i in (2 * k, 2 * k + 1):
                    gather(it, i, table, L_ix, L_stash, L_get)
                for j in range(steps):
                    s, m = h * 2 + j, 2 * k + j
                    p = part_of(s)
                    pool.wait_ge(L_h.sem, L_h.after(s))
                    nc.gpsimd.tensor_tensor(x2[m][0:p, :], x2[m][0:p, :], xc[m][0:p, :], ALU.add)\
                        .then_inc(L_yy.sem, 1)

            for k in range(4):
                half2(k // 2, k % 2, 2, 2)
            with pool.Fori(2, BODY) as it:
                for k in range(2):
                    half2(it, k, 2, 2)
            half2(BODY, 0, 1, 2)
            for q in range(2):
                pool.wait_ge(L_st.sems[q], L_st.after((NS - q) // 2))
            groups(scatter, out, L_px, L_put)

        @block.vector
        def _(dve):
            V = nc.vector

            def inverse_sqrt(total, tmp, n_mean, eps, done):
                v, y, a = tmp
                done(V.tensor_scalar(v, total, n_mean, eps, ALU.mult, ALU.add))
                done(V.tensor_scalar(y.bitcast(I32), v.bitcast(I32), -0.5, MAGIC, ALU.mult, ALU.add))
                for _ in range(3):
                    done(V.scalar_tensor_tensor(out=a, in0=y, scalar=-0.5, in1=y, op0=ALU.mult, op1=ALU.mult))
                    done(V.tensor_tensor(a, a, v, ALU.mult))
                    done(V.scalar_tensor_tensor(out=y, in0=a, scalar=1.5, in1=y, op0=ALU.add, op1=ALU.mult))

            def in_stage(st, step):
                k = [0]

                def done(ins):
                    k[0] += 1
                    ins.then_inc(st.sem, 1)
                    dve.wait_ge(st.sem, st.after(step, k[0]))
                return done

            V.memset(wres2[:, :], 0.0)
            V.memset(wconv[:, :], 0.0)
            V.memset(wm2[:, :], 0.0)
            V.memset(bias_in[:, :, :], 0.0)
            V.memset(bias16[:, :, :, :], 0.0)
            V.memset(stat[:, :, :], 1.0)
            V.memset(shift[:, :], -SHIFT)
            for q in range(2):
                V.memset(res[q][:, :, P:P + 1], 1.0)
            V.memset(end_mark[:, :], -1).then_inc(s_v, 1)
            dve.wait_ge(s_v, 1)
            dve.wait_ge(s_w, 16 * 23)
            V.memset(wconv[D:D + 1, D:D + 1], 1.0)
            V.tensor_copy(bias_part[:, 0, :, :], bias_in[:, :, :]).then_inc(s_v, 1)
            dve.wait_ge(s_v, 2)
            dve.wait_ge(s_flat, 48)
            V.tensor_tensor(same_flat[:, :], flat[:, 0, :], flat[:, 1, :], ALU.is_equal).then_inc(s_v, 1)
            V.tensor_tensor(last[:, :], dst_idx[:, :], next_idx[:, :], ALU.is_equal).then_inc(s_bnd, 1)
            dve.wait_ge(s_bnd, 1)
            dve.wait_ge(s_dst, 16)
            V.scalar_tensor_tensor(out=put_idx[:, :], in0=last[:, :], scalar=float(BEYOND), in1=dst_idx[:, :],
                                   op0=ALU.mult, op1=ALU.add).then_inc(s_v, 1)
            dve.wait_ge(s_v, 4)
            V.tensor_scalar(last[:, :], last[:, :], -1.0, 1.0, ALU.mult, ALU.add).then_inc(s_v, 1)
            for i in range(2):
                V.tensor_tensor(bias_rest[:, i, :, :], bias_in[:, :, :] if i == 0 else bias_rest[:, 0, :, :],
                                bias_part[:, i, :, :], ALU.subtract).then_inc(s_v, 1)
                dve.wait_ge(s_v, 6 + 2 * i)
                V.tensor_copy(bias_part[:, i + 1, :, :], bias_rest[:, i, :, :]).then_inc(s_v, 1)
                dve.wait_ge(s_v, 7 + 2 * i)
            for i in range(3):
                for b in range(2):
                    V.tensor_copy(bias16[32 * i:32 * i + 1, b, :, :],
                                  cols(bias_part[32 * i:32 * i + 1, i, b, :], 8)).then_inc(s_v, 1)

            def sum_squares(total, squares, squared, step, st):
                squared.done(dve, step)
                V.tensor_reduce(total, rows(squares), AX, ALU.add).then_inc(st.sem, 1)

            def invert(h, steps, dense_sums, edge_sums, st):
                if steps:
                    dve.wait_ge(dense_sums.sem, dense_sums.after(h * 2 + (1 if steps == 2 else 0)))
                    p, c = P, 0
                else:
                    p, c = EP, 2 * R
                if in_range(h):
                    dve.wait_ge(edge_sums.sem, edge_sums.after(h))
                inverse_sqrt(stat[0:p, 1, c:], tuple(stat[0:p, i, c:] for i in (2, 3, 4)), 1.0 / D, LN_EPS,
                             in_stage(st, h))

            def subtract_mean(tile, source, total, st, step, k):
                V.tensor_reduce(total, rows(source), AX, ALU.add).then_inc(st.sem, 1)
                dve.wait_ge(st.sem, st.after(step, k))
                V.scalar_tensor_tensor(out=rows(tile), in0=per_row(total), scalar=-1.0 / D, in1=rows(source),
                                       op0=ALU.mult, op1=ALU.add).then_inc(st.sem, 1)

            def relu_scale(tile, source, deviation, st):
                V.scalar_tensor_tensor(out=tile, in0=source, scalar=0.0, in1=per_row(deviation), op0=ALU.max,
                                       op1=ALU.mult).then_inc(st.sem, 1)

            def center(s, turn, j, m):
                dve.wait_ge(S_x.sems[j], S_x.after(turn))
                S_t.done(dve, s - 4)
                p = part_of(s)
                subtract_mean(xc[m][0:p, :], xin[j][0:p, :], stat[0:p, 0, j * R:j * R + R], S_center, s, 1)

            def edge_center(g, it, k):
                dve.wait_ge(S_eg.sems[k], S_eg.after(it))
                S_et.done(dve, g - 2)
                subtract_mean(ec[k][:, :], eg[k][:, :], stat[0:EP, 0, 2 * R:], S_ea, g, 1)

            def edge_score(g, k):
                w = EJ * D
                relu_scale(rows(ec[k][:, :]), rows(ec[k][:, :]), stat[0:EP, 3, 2 * R:], S_eb)
                dve.wait_ge(S_eb.sem, S_eb.after(g, 1))
                V.tensor_tensor(prod[:, :], ec[k][:, 0:w], ec[k][:, w:2 * w], ALU.mult).then_inc(S_eb.sem, 1)
                dve.wait_ge(S_eb.sem, S_eb.after(g, 2))
                S_exp.done(dve, g - 1)
                V.tensor_reduce(score[:, :], rows(prod[:, :]), AX, ALU.add).then_inc(S_eb.sem, 1)

            def edge_weight(g, k):
                dve.wait_ge(S_exp.sem, S_exp.after(g))
                V.tensor_tensor(weighted[:, :, 0:D], rows(ec[k][:, 0:EJ * D]), per_row(weighted[:, :, D]),
                                ALU.mult).then_inc(S_ew.sem, 1)

            def edge_scan(g, turn, q):
                dve.wait_ge(S_et.sem, S_et.after(g))
                dve.wait_ge(S_same.sems[q], S_same.after(turn))
                S_agg.done(dve, g - 2)
                if isinstance(g, int) and g == 0:
                    carry = 0.0
                else:
                    S_scan.done(dve, g - 1)
                    carry = sums[1 - q][:, EG - 1:EG]
                V.tensor_tensor_scan(sums[q][:, :], same[q][0:D + 1, :], bank_w[0:D + 1, 0:EG], carry,
                                     ALU.mult, ALU.add).then_inc(S_scan.sem, 1)

            def edge_finish(g, bank):
                dve.wait_ge(S_agg.sem, S_agg.after(g))
                dve.wait_ge(S_rd.sem, S_rd.after(g))
                S_es.done(dve, g - 1)
                acc = bank[0:EP, 0:EJ * (D + 1)].rearrange("p (j d) -> p j d", d=D + 1)
                V.reciprocal(inv[:, :], acc[:, :, D]).then_inc(S_ee.sem, 1)
                dve.wait_ge(S_ee.sem, S_ee.after(g, 1))
                V.tensor_tensor(diff[:, :, 0:D], acc[:, :, 0:D], per_row(inv[:, :]), ALU.mult)\
                 .then_inc(S_ee.sem, 1)
                dve.wait_ge(S_ee.sem, S_ee.after(g, 2))
                here = group_cols(dst_rows, g)
                V.tensor_tensor(rows(here), diff[:, :, 0:D], rows(rdst[:, :]), ALU.add).then_inc(S_ee.sem, 1)
                dve.wait_ge(S_ee.sem, S_ee.after(g, 3))
                V.tensor_tensor(twice[:, :], here, rdst[:, :], ALU.add).then_inc(S_ee.sem, 1)
                dve.wait_ge(S_ee.sem, S_ee.after(g, 4))
                V.tensor_tensor(diff[:, :, D:2 * D], diff[:, :, 0:D], rows(twice[:, :]), ALU.mult)\
                 .then_inc(S_ee.sem, 1)

            def half1(it, k, steps, before):
                h = it * 2 + k
                if steps:
                    center(h * 2, h, 0, 2 * k)
                if steps == 2:
                    center(h * 2 + 1, h, 1, 2 * k + 1)
                if in_range(h - 1):
                    edge_weight(h - 1, 1 - k)
                if in_range(h):
                    edge_center(h, it, k)
                for j in range(steps):
                    s = h * 2 + j
                    p = part_of(s)
                    sum_squares(stat[0:p, 1, j * R:j * R + R], sq[j][0:p, :], S_sq, s, S_ss)
                if in_range(h):
                    sum_squares(stat[0:EP, 1, 2 * R:], esq[:, :], S_esq, h, S_ess)
                    invert(h, steps, S_ss, S_ess, S_inv)
                for j in range(steps):
                    s = h * 2 + j
                    p = part_of(s)
                    t_ = rows(xc[2 * k + j][0:p, :])
                    relu_scale(t_, t_, stat[0:p, 3, j * R:j * R + R], S_h)
                if in_range(h):
                    edge_score(h, k)
                if in_range(h - 1):
                    edge_scan(h - 1, it - 1 + k, 1 - k)
                if in_range(h - 2):
                    edge_finish(h - 2, products_banks(k, steps or before)[0])

            halves(dve.Fori, half1)

            dve.wait_ge(S_es.sem, S_es.after(G))
            c = [1]

            def link(ins):
                c[0] += 1
                ins.then_inc(s_bnd, 1)
                dve.wait_ge(s_bnd, c[0])

            link(V.tensor_tensor(bndiag[:, :], bank_sum[:, 0:P], ident[:, :], ALU.mult))
            link(V.tensor_reduce(bncol[:, 0:1], bndiag[:, :], AX, ALU.add))
            link(V.tensor_copy(bncol[:, 1:3], bank_sum[:, P:P + 2]))
            link(V.tensor_tensor(bndiag[:, 0:D], ident[:, 0:D], ident[:, D:P], ALU.add))
            link(V.tensor_scalar(bnz[:, 0, 0, :], bndiag[:, 0:D], bncol[:, 1:2], None, ALU.mult))
            link(V.tensor_scalar(bnz[:, 0, 1, :], bndiag[:, 0:D], bncol[:, 0:1], None, ALU.mult))
            link(V.tensor_scalar(bnz[:, 1, :, :].rearrange("p a d -> p (a d)"), ident[:, :], bncol[:, 2:3],
                                 None, ALU.mult))
            assert c[0] == BN_PARTS
            dve.wait_ge(s_bnp, 1)
            mean, m2, var, v_, y_, a_, tmp = (bnw[:, i, :] for i in range(7))
            link(V.tensor_scalar(bnw[:, 0:2, :].rearrange("p a d -> p (a d)"), bank_r[0][:, 0:2 * D], 1.0 / N,
                                 None, ALU.mult))
            link(V.tensor_tensor(tmp, mean, mean, ALU.mult))
            link(V.tensor_tensor(var, m2, tmp, ALU.subtract))
            inverse_sqrt(var, (v_, y_, a_), 1.0, BN_EPS, link)
            link(V.tensor_tensor(bn[:, 0, :], bn_in[:, 0, :], y_, ALU.mult))
            link(V.tensor_tensor(tmp, mean, bn[:, 0, :], ALU.mult))
            link(V.tensor_tensor(bn[:, 1, :], bn_in[:, 1, :], tmp, ALU.subtract))

            def x2_scale(tile, row, n, st):
                V.tensor_tensor(rows(tile), rows(row), cols(bn[0:tile.shape[0], 0, :], n), ALU.mult)\
                 .then_inc(st.sem, 1)

            def x2_add(tile, xrow, st, step):
                dve.wait_ge(st.sem, st.after(step, 1))
                V.tensor_tensor(tile, tile, xrow, ALU.add).then_inc(st.sem, 1)

            def x2_center(tile, mid, n, total, st, step):
                dve.wait_ge(st.sem, st.after(step, 2))
                V.tensor_tensor(rows(tile), rows(tile), cols(bn[0:tile.shape[0], 1, :], n), ALU.add)\
                 .then_inc(st.sem, 1)
                dve.wait_ge(st.sem, st.after(step, 3))
                subtract_mean(mid, tile, total, st, step, 4)

            def dense_x2_begin(s, turn, j, m):
                dve.wait_ge(L_x.sems[j], L_x.after(turn))
                L_t.done(dve, s - 4)
                L_yy.done(dve, s - 4)
                L_y.done(dve, s - 4)
                p = part_of(s)
                x2_scale(x2[m][0:p, :], rin[j][0:p, :], R, L_f)
                x2_add(x2[m][0:p, :], xin[j][0:p, :], L_f, s)

            def dense_x2_end(s, j, m):
                p = part_of(s)
                x2_center(x2[m][0:p, :], xc[m][0:p, :], R, stat[0:p, 0, j * R:j * R + R], L_f, s)

            def edge_x2(g, it, k):
                dve.wait_ge(M_ld.sems[k], M_ld.after(it))
                M_b.done(dve, g - 1)
                x2_scale(ex[:, :], er[k][:, :], 2 * EJ, M_a)
                x2_add(ex[:, :], eg[k][:, :], M_a, g)
                x2_center(ex[:, :], ec[0][:, :], 2 * EJ, stat[0:EP, 0, 2 * R:], M_a, g)

            def edge_h2(g, k):
                w = EJ * D
                M_t.done(dve, g - 1)
                relu_scale(hsrc[k][:, :, 0:D], rows(ec[0][:, 0:w]), stat[0:EP, 3, 2 * R:2 * R + EJ], M_b)
                relu_scale(rows(hdst[:, :]), rows(ec[0][:, w:2 * w]), stat[0:EP, 3, 2 * R + EJ:], M_b)
                dve.wait_ge(M_b.sem, M_b.after(g, 2))
                V.tensor_tensor(group_cols(dst_rows, g), ex[:, w:2 * w], hdst[:, :], ALU.add)\
                 .then_inc(M_b.sem, 1)

            def edge_scan2(g, turn, q):
                dve.wait_ge(M_g2.sem, M_g2.after(g))
                dve.wait_ge(M_same.sems[q], M_same.after(turn))
                M_c.done(dve, g - 2)
                if isinstance(g, int) and g == 0:
                    carry = 0.0
                else:
                    M_scan.done(dve, g - 1)
                    carry = pairT[1 - q][D:P, EG - 1:EG]
                V.tensor_tensor_scan(pairT[q][D:P, :], same[q][D:P, :], m2T[D:P, :], carry,
                                     ALU.mult, ALU.add).then_inc(M_scan.sem, 1)

            def edge_final(g):
                dve.wait_ge(M_og.sem, M_og.after(g))
                dve.wait_ge(M_b.sem, M_b.after(g))
                here = group_cols(dst_rows, g)
                V.tensor_tensor(here, here, eadd[:, :], ALU.add).then_inc(M_y.sem, 1)

            def final_rows(s, j, m):
                dve.wait_ge(L_og.sem, L_og.after(s))
                dve.wait_ge(L_yy.sem, L_yy.after(s))
                p = part_of(s)
                here = res[j][0:p, :, 0:P]
                V.tensor_tensor(here, pairs(x2[m][0:p, :]), here, ALU.add).then_inc(L_y.sem, 1)

            def finals(h, k, j, steps, before):
                s = h * 2 - 4 + j
                if (steps or before) and not (isinstance(s, int) and s < 0):
                    final_rows(s, j, (2 * k + j) % 4)
                if not steps and before and j:
                    final_rows(NS, 0, NS % 4)

            def half2(it, k, steps, before):
                h = it * 2 + k
                finals(h, k, 0, steps, before)
                if steps:
                    dense_x2_begin(h * 2, h, 0, 2 * k)
                if in_range(h - 2):
                    edge_scan2(h - 2, it - 1, k)
                if steps:
                    dense_x2_end(h * 2, 0, 2 * k)
                if in_range(h):
                    edge_x2(h, it, k)
                if steps == 2:
                    sum_squares(stat[0:P, 1, 0:R], sq[0][:, :], L_sq, h * 2, L_ss)
                finals(h, k, 1, steps, before)
                if steps == 2:
                    dense_x2_begin(h * 2 + 1, h, 1, 2 * k + 1)
                    dense_x2_end(h * 2 + 1, 1, 2 * k + 1)
                if steps == 1:
                    sum_squares(stat[0:PT, 1, 0:R], sq[0][0:PT, :], L_sq, NS, L_ss)
                if in_range(h):
                    sum_squares(stat[0:EP, 1, 2 * R:], esq[:, :], M_sq, h, M_ss)
                if steps == 2:
                    sum_squares(stat[0:P, 1, R:2 * R], sq[1][:, :], L_sq, h * 2 + 1, L_ss)
                if in_range(h):
                    invert(h, steps, L_ss, M_ss, L_inv)
                for j in range(steps):
                    p = part_of(h * 2 + j)
                    t_ = rows(xc[2 * k + j][0:p, :])
                    relu_scale(t_, t_, stat[0:p, 3, j * R:j * R + R], L_h)
                if in_range(h):
                    edge_h2(h, k)
                if in_range(h - 2):
                    edge_final(h - 2)

            halves(dve.Fori, half2)

        @block.scalar
        def _(act):
            A = nc.scalar

            def blocks(a, p):
                return a if p == P else a.rearrange("f (k n) -> f k n", n=P)[:, :, 0:p]

            def square(s, j, m, ready, summed, st):
                act.wait_ge(ready.sem, ready.after(s))
                summed.done(act, s - 2)
                p = part_of(s)
                A.activation(sq[j][0:p, :], xc[m][0:p, :], ACT.Square).then_inc(st.sem, 1)

            def edge_square(g, tile, ready, summed, st):
                act.wait_ge(ready.sem, ready.after(g))
                summed.done(act, g - 1)
                A.activation(esq[:, :], tile, ACT.Square).then_inc(st.sem, 1)

            def copy_hT(u, bank, ready, read, st):
                s, b, p = u.s, u.b, part_of(u.s)
                act.wait_ge(ready.sem, ready.after(s, b + 1))
                read.part(act, s - 1, b + 1)
                A.activation(blocks(hT[:, b * 512:b * 512 + 512], p), blocks(bank[:, :], p), ACT.Copy)\
                 .then_inc(st.sem, 1)

            def relu_r(u):
                s, b, p = u.s, u.b, part_of(u.s)
                act.wait_ge(S_r.sem, S_r.after(s, b + 1))
                if b == 0:
                    S_gram.done(act, s - 2)
                    S_st.done(act, u.turn - 1, u.j)
                A.activation(res[u.j][0:p, 4 * b:4 * b + 4, 0:P], pairs(bank_r[b][0:p, :]), ACT.Relu)\
                 .then_inc(S_relu.sem, 1)

            def slot1(h, k, n, before):
                u = unit(h, k, n)
                if n < 2 * before:
                    copy_hT(u, bank_t[u.b], S_t, S_r, S_ht)
                u = unit(h, k, n - 1)
                if in_work(u, n - 1, before):
                    relu_r(u)

            def edge_exp(g):
                act.wait_ge(S_eb.sem, S_eb.after(g))
                S_et.done(act, g - 1)
                A.activation(weighted[:, :, D], score[:, :], ACT.Exp, bias=shift[0:EP, :])\
                 .then_inc(S_exp.sem, 1)

            def copy_hdT(g):
                act.wait_ge(S_et.sem, S_et.after(g))
                S_agg.done(act, g - 1)
                A.activation(hdT[:, :], bank_d[0:D, 0:EG], ACT.Copy).then_inc(S_hd.sem, 1)

            def relu_dst(g, bank):
                act.wait_ge(S_agg.sem, S_agg.after(g))
                S_ee.done(act, g - 1)
                A.activation(rdst[:, :], bank[0:EP, 0:EJ * D], ACT.Relu).then_inc(S_rd.sem, 1)

            def half1(it, k, steps, before):
                h = it * 2 + k
                if in_range(h - 1):
                    edge_exp(h - 1)
                if steps:
                    square(h * 2, 0, 2 * k, S_center, S_ss, S_sq)
                elif in_range(h):
                    edge_square(h, ec[k][:, :], S_ea, S_ess, S_esq)
                if in_range(h - 2):
                    relu_dst(h - 2, products_banks(k, steps or before)[1])
                if steps == 2:
                    square(h * 2 + 1, 1, 2 * k + 1, S_center, S_ss, S_sq)
                slot1(h, k, 0, before)
                if steps and in_range(h):
                    edge_square(h, ec[k][:, :], S_ea, S_ess, S_esq)
                slot1(h, k, 1, before)
                if in_range(h - 1):
                    copy_hdT(h - 1)
                slot1(h, k, 2, before)
                slot1(h, k, 3, before)

            act.wait_ge(s_v, 1)
            halves(act.Fori, half1)

            act.wait_ge(s_w, 16 * 23)

            def gelu_c(u):
                s, b, p = u.s, u.b, part_of(u.s)
                act.wait_ge(L_c.sem, L_c.after(s, b + 1))
                L_o.part(act, s - 1, b + 1)
                for i in range(2):
                    ins = A.activation(blocks(cT[b][:, i, :], p), blocks(bank_c[b][i][0:H2, :], p), ACT.Gelu,
                                       bias=bc1[:, :])
                ins.then_inc(L_cg.sem, 1)

            def gelu_out(u):
                s, b, p = u.s, u.b, part_of(u.s)
                act.wait_ge(L_o.sem, L_o.after(s, b + 1))
                if b == 0:
                    L_st.done(act, u.turn - 1, u.j)
                A.activation(res[u.j][0:p, 4 * b:4 * b + 4, 0:P], pairs(bank_o[0:p, :]), ACT.Gelu)\
                 .then_inc(L_og.sem, 1)

            def block_hT(h, k, n, before):
                if n < 2 * before:
                    copy_hT(unit(h, k, n), bank_h, L_t, L_c, L_ht)

            def block_c(h, k, n, before):
                u = unit(h, k, n - 1)
                if in_work(u, n - 1, before):
                    gelu_c(u)

            def block_out(h, k, n, before):
                u = unit(h, k, n - 2)
                if in_work(u, n - 2, before):
                    gelu_out(u)

            def edge_copies(g, q):
                act.wait_ge(M_t.sem, M_t.after(g, 1))
                M_m1.done(act, g - 1)
                A.activation(restT[:, :], bank_y[0:D + DE, 0:EG], ACT.Copy).then_inc(M_tc.sem, 1)
                act.wait_ge(M_t.sem, M_t.after(g, 2))
                M_c.done(act, g - 2)
                A.activation(pairT[q][0:D, :], bank_x[0:D, 0:EG], ACT.Copy).then_inc(M_tc.sem, 1)

            def edge_gelu1(g):
                act.wait_ge(M_m1.sem, M_m1.after(g))
                M_m2.done(act, g - 1)
                A.activation(m1T[:, :], bank_y[0:H1, 0:EG], ACT.Gelu, bias=bm1[:, :]).then_inc(M_g1.sem, 1)

            def edge_gelu2(g):
                act.wait_ge(M_m2.sem, M_m2.after(g))
                M_scan.done(act, g - 1)
                A.activation(m2T[D:P, :], bank_x[D:P, 0:EG], ACT.Gelu, bias=bm2[D:P, :]).then_inc(M_g2.sem, 1)

            def edge_gelu_c(g, drain):
                act.wait_ge(M_c.sem, M_c.after(g))
                M_o.done(act, g - 1)
                A.activation(ecT[:, :], (bank_h if drain else bank_y)[0:H2, 0:EG], ACT.Gelu, bias=bc1[:, :]).then_inc(M_cg.sem, 1)

            def edge_gelu_out(g, drain):
                act.wait_ge(M_o.sem, M_o.after(g))
                M_y.done(act, g - 1)
                A.activation(eadd[:, :], (bank_o if drain else bank_x)[0:EP, 0:EJ * D], ACT.Gelu).then_inc(M_og.sem, 1)

            def half2(it, k, steps, before):
                h = it * 2 + k
                drain = not steps and not before
                if drain:
                    if in_range(h - 1):
                        edge_copies(h - 1, 1 - k)
                    if in_range(h - 2):
                        edge_gelu_c(h - 2, drain)
                    if in_range(h):
                        edge_square(h, ec[0][:, :], M_a, M_ss, M_sq)
                    if in_range(h - 1):
                        edge_gelu1(h - 1)
                    if in_range(h - 2):
                        edge_gelu_out(h - 2, drain)
                    if in_range(h - 1):
                        edge_gelu2(h - 1)
                    return
                block_hT(h, k, 0, before)
                if in_range(h - 2):
                    edge_gelu2(h - 2)
                block_c(h, k, 0, before)
                block_out(h, k, 0, before)
                block_hT(h, k, 1, before)
                if steps:
                    square(h * 2, 0, 2 * k, L_f, L_ss, L_sq)
                if in_range(h - 2):
                    edge_gelu_c(h - 2, drain)
                block_c(h, k, 1, before)
                block_out(h, k, 1, before)
                block_hT(h, k, 2, before)
                if in_range(h - 2):
                    edge_gelu_out(h - 2, drain)
                block_c(h, k, 2, before)
                edge_square(h, ec[0][:, :], M_a, M_ss, M_sq)
                if in_range(h - 1):
                    edge_copies(h - 1, 1 - k)
                block_out(h, k, 2, before)
                block_hT(h, k, 3, before)
                if steps == 2:
                    square(h * 2 + 1, 1, 2 * k + 1, L_f, L_ss, L_sq)
                if in_range(h - 1):
                    edge_gelu1(h - 1)
                block_c(h, k, 3, before)
                block_out(h, k, 3, before)
                if before and not steps:
                    edge_gelu2(h - 1)

            halves(act.Fori, half2)

        @block.tensor
        def _(pe):
            T = nc.tensor
            pe.wait_ge(s_v, 15)
            pe.wait_ge(s_c, 2)
            pe.wait_ge(s_w, 16 * 23)
            b_res = bias16[:, 0, :, :].rearrange("p r d -> p (r d)")
            b_out = bias16[:, 1, :, :].rearrange("p r d -> p (r d)")

            def zero_sums(start, stop):
                return T.matmul(bank_sum[:, :], wm2[:, 0:1].broadcast_to([H1, P]),
                                ones[0:H1, 0:1].broadcast_to([H1, 512]), start=start, stop=stop)

            zero_sums(True, False).then_inc(s_zero, 1)

            def transpose_h(u, bank, ready, st):
                p = part_of(u.s)
                pe.wait_ge(ready.sem, ready.after(u.s))
                for i in range(4):
                    c = (4 * u.b + i) * P
                    ins = T.transpose(bank[:, i * P:i * P + p], xc[u.m][0:p, c:c + P], ident[0:p, 0:p])
                ins.then_inc(st.sem, 1)

            def add_sums(u):
                p = part_of(u.s)
                pe.wait_ge(S_relu.sem, S_relu.after(u.s, u.b + 1))
                for i in range(4 * u.b, 4 * u.b + 4):
                    ins = T.matmul(bank_sum[:, 0:P + 1], res[u.j][0:p, i, 0:P], res[u.j][0:p, i, :],
                                   start=False, stop=False)
                ins.then_inc(S_gram.sem, 1)

            def r_product(u):
                s, b, p = u.s, u.b, part_of(u.s)
                pe.wait_ge(S_ht.sem, S_ht.after(s, b + 1))
                S_relu.part(pe, s - 1, b + 1)
                for i in range(4):
                    c = (4 * b + i) * P
                    T.matmul(bank_r[b][0:p, i * P:i * P + P], hT[:, c:c + p], wres2[:, :],
                             start=(i == 0), stop=False)
                T.matmul(bank_r[b][0:p, :], ones16[:, 0:p], b_res, start=False, stop=True)\
                 .then_inc(S_r.sem, 1)

            def slot1(h, k, n, before, edges=None, *args):
                if n < 2 * before:
                    u = unit(h, k, n)
                    S_ht.part(pe, u.s - 1, u.b + 1)
                    transpose_h(u, bank_t[u.b], S_h, S_t)
                if edges:
                    edges(*args)
                for back, do in ((1, r_product), (2, add_sums)):
                    u = unit(h, k, n - back)
                    if in_work(u, n - back, before):
                        do(u)

            def edge_transposes(g, k, dense):
                pe.wait_ge(S_ew.sem, S_ew.after(g))
                S_scan.done(pe, g - 1)
                (S_rd if dense else S_hd).done(pe, g - 1)
                for j in range(EJ):
                    T.transpose(bank_w[0:D + 1, j:EG:EJ], weighted[:, j, :], ident[0:EP, 0:EP])
                    ins = T.transpose(bank_d[0:D, j:EG:EJ], ec[k][:, (EJ + j) * D:(EJ + j + 1) * D],
                                      ident[0:EP, 0:EP])
                ins.then_inc(S_et.sem, 1)

            def edge_products(g, q, dense):
                bank_a, bank_d = products_banks(q, dense)
                pe.wait_ge(S_scan.sem, S_scan.after(g))
                pe.wait_ge(S_hd.sem, S_hd.after(g))
                if dense:
                    S_ee.done(pe, g - 1)
                else:
                    S_ee.done(pe, g - 2)
                    S_rd.done(pe, g - 1)
                for j in range(EJ):
                    ins = T.matmul(bank_a[0:EP, j * (D + 1):(j + 1) * (D + 1)], sums[q][:, j:EG:EJ],
                                   wconv[:, :], start=(j == 0), stop=(j == EJ - 1))
                ins.then_inc(S_agg.sem, 1)
                for j in range(EJ):
                    T.matmul(bank_d[0:EP, j * D:(j + 1) * D], hdT[:, j:EG:EJ], wres2[0:D, 0:D],
                             start=(j == 0), stop=False)
                T.matmul(bank_d[0:EP, 0:EJ * D], ones16[:, 0:EP], b_res[:, 0:EJ * D], start=False, stop=True)\
                 .then_inc(S_agg.sem, 1)

            def edge_stats(g):
                pe.wait_ge(S_ee.sem, S_ee.after(g))
                for j in range(EJ):
                    c = last[:, g * EJ + j:g * EJ + j + 1] if isinstance(g, int) else \
                        last[:, bass.ds(g * EJ + j, 1)]
                    ins = T.matmul(bank_sum[:, P + 1:P + 2], diff[:, j, :], c, start=False, stop=False)
                ins.then_inc(S_es.sem, 1)

            def half1(it, k, steps, before):
                h = it * 2 + k
                if in_range(h - 2):
                    edge_products(h - 2, k, steps or before)
                slot1(h, k, 0, before)
                if in_range(h - 1):
                    slot1(h, k, 1, before, edge_transposes, h - 1, 1 - k, steps or before)
                else:
                    slot1(h, k, 1, before)
                if in_range(h - 3):
                    edge_stats(h - 3)
                slot1(h, k, 2, before)
                slot1(h, k, 3, before)
                if before and not steps:
                    pe.wait_ge(S_ht.sem, S_ht.after(NS))
                    pe.wait_ge(S_relu.sem, S_relu.after(NS))

            pe.wait_ge(s_zero, 1)
            halves(pe.Fori, half1)
            edge_stats(G - 1)
            zero_sums(False, True).then_inc(S_es.sem, 1)

            pe.wait_ge(s_bnd, BN_PARTS)
            T.matmul(bank_r[0][:, 0:P], ones[:, :], bnz[:, 0, :, :].rearrange("p a d -> p (a d)"),
                     start=True, stop=False)
            T.matmul(bank_r[0][:, 0:P], ones[:, :], bnz[:, 1, :, :].rearrange("p a d -> p (a d)"),
                     start=False, stop=True).then_inc(s_bnp, 1)
            pe.wait_ge(s_bnd, BN_PARTS + 1)

            def c_product(u):
                s, b, p = u.s, u.b, part_of(u.s)
                pe.wait_ge(L_ht.sem, L_ht.after(s, b + 1))
                L_cg.part(pe, s - 1, b + 1)
                for i in range(2):
                    o = bank_c[b][i][0:H2, :]
                    a = hT[i * D:i * D + D, b * 512:b * 512 + 512]
                    if p != P:
                        o = o.rearrange("f (k n) -> f k n", n=P)[:, :, 0:p]
                        a = a.rearrange("f (k n) -> f k n", n=P)[:, :, 0:p]
                    ins = T.matmul(o, wc1_node[i * D:i * D + D, :], a, start=True, stop=True)
                ins.then_inc(L_c.sem, 1)

            def out_product(u):
                s, b, p = u.s, u.b, part_of(u.s)
                pe.wait_ge(L_cg.sem, L_cg.after(s, b + 1))
                if b:
                    pe.wait_ge(L_og.sem, L_og.after(s, 1))
                else:
                    L_og.done(pe, s - 1)
                for i in range(8):
                    T.matmul(bank_o[0:p, i * D:i * D + D], cT[b][:, i % 2, (i // 2) * P:(i // 2) * P + p],
                             wc2[:, :], start=(i == 0), stop=False)
                T.matmul(bank_o[0:p, :], ones16[:, 0:p], b_out, start=False, stop=True).then_inc(L_o.sem, 1)

            def block_c(h, k, n, before):
                u = unit(h, k, n - 1)
                if in_work(u, n - 1, before):
                    c_product(u)

            def block_out(h, k, n, before):
                u = unit(h, k, n - 2)
                if in_work(u, n - 2, before):
                    out_product(u)

            def block_t(h, k, n, before):
                if n < 2 * before:
                    u = unit(h, k, n)
                    if u.b:
                        pe.wait_ge(L_ht.sem, L_ht.after(u.s, 1))
                    else:
                        L_ht.done(pe, u.s - 1)
                    transpose_h(u, bank_h, L_h, L_t)

            def edge_transposes2(g, q, read_y, read_x):
                pe.wait_ge(M_b.sem, M_b.after(g, 2))
                read_y.done(pe, g - 1)
                read_x.done(pe, g - 1)
                for j in range(EJ):
                    ins = T.transpose(bank_y[0:D + DE, j:EG:EJ], hsrc[q][:, j, :], ident[0:EP, 0:EP])
                ins.then_inc(M_t.sem, 1)
                for j in range(EJ):
                    ins = T.transpose(bank_x[0:D, j:EG:EJ], hdst[:, j * D:j * D + D], ident[0:EP, 0:EP])
                ins.then_inc(M_t.sem, 1)

            def edge_message1(g, q):
                pe.wait_ge(M_tc.sem, M_tc.after(g))
                T.matmul(bank_y[0:H1, 0:EG], wm1_rest[:, :], restT[:, :], start=True, stop=False)
                T.matmul(bank_y[0:H1, 0:EG], wm1_dst[:, :], pairT[q][0:D, :], start=False, stop=True)\
                 .then_inc(M_m1.sem, 1)

            def edge_message2(g):
                pe.wait_ge(M_g1.sem, M_g1.after(g))
                T.matmul(bank_x[:, 0:EG], wm2[:, :], m1T[:, :], start=True, stop=True).then_inc(M_m2.sem, 1)

            def edge_c(g, q, drain):
                pe.wait_ge(M_scan.sem, M_scan.after(g))
                if drain:
                    M_cg.done(pe, g - 1)
                T.matmul((bank_h if drain else bank_y)[0:H2, 0:EG], wc1[:, :], pairT[q][:, :], start=True, stop=True)\
                 .then_inc(M_c.sem, 1)

            def edge_out(g, drain):
                bank = bank_o if drain else bank_x
                if drain:
                    M_og.done(pe, g - 1)
                else:
                    pe.wait_ge(M_g2.sem, M_g2.after(g))
                pe.wait_ge(M_cg.sem, M_cg.after(g))
                for j in range(EJ):
                    T.matmul(bank[0:EP, j * D:(j + 1) * D], ecT[:, j:EG:EJ], wc2[:, :],
                             start=(j == 0), stop=False)
                T.matmul(bank[0:EP, 0:EJ * D], ones16[:, 0:EP], b_out[:, 0:EJ * D], start=False, stop=True)\
                 .then_inc(M_o.sem, 1)

            def half2(it, k, steps, before):
                h = it * 2 + k
                drain = not steps and not before
                if drain:
                    if in_range(h - 1):
                        edge_transposes2(h - 1, 1 - k, M_g1, M_g2)
                    if in_range(h - 2):
                        edge_c(h - 2, k, drain)
                    if in_range(h - 1):
                        edge_message1(h - 1, 1 - k)
                    if in_range(h - 2):
                        edge_out(h - 2, drain)
                    if in_range(h - 1):
                        edge_message2(h - 1)
                    return
                block_t(h, k, 0, before)
                if in_range(h - 2):
                    edge_message2(h - 2)
                block_c(h, k, 0, before)
                block_out(h, k, 0, before)
                block_t(h, k, 1, before)
                if in_range(h - 2):
                    edge_c(h - 2, k, drain)
                block_c(h, k, 1, before)
                block_out(h, k, 1, before)
                block_t(h, k, 2, before)
                if in_range(h - 2):
                    edge_out(h - 2, drain)
                block_c(h, k, 2, before)
                if in_range(h - 1):
                    edge_transposes2(h - 1, 1 - k, M_cg, M_og)
                block_out(h, k, 2, before)
                block_t(h, k, 3, before)
                if in_range(h - 1):
                    edge_message1(h - 1, 1 - k)
                block_c(h, k, 3, before)
                block_out(h, k, 3, before)
                if before and not steps:
                    edge_message2(h - 1)

            halves(pe.Fori, half2)


_INS = ["x", "src", "dst", "edge_attr_32", "L0_gnn_W_conv", "L0_gnn_b_conv", "L0_gnn_W_res", "L0_gnn_b_res",
        "L0_gnn_gamma", "L0_gnn_beta", "L1_gnn_W_m1", "L1_gnn_b_m1", "L1_gnn_W_m2", "L1_gnn_b_m2",
        "L1_gnn_W_c1", "L1_gnn_b_c1", "L1_gnn_W_c2", "L1_gnn_b_c2"]


def kernel(**inputs):
    import numpy as np
    import concourse.bacc as bacc
    from concourse.bass_utils import run_bass_kernel_spmd as run

    nc = bacc.Bacc("TRN2", target_bir_lowering=False, num_devices=1)
    arrays, aps = {}, {}
    for name in _INS:
        a = np.ascontiguousarray(inputs[name])
        arrays[f"in_{name}"] = a
        aps[name] = nc.dram_tensor(f"in_{name}", a.shape, mybir.dt.from_np(a.dtype), kind="ExternalInput").ap()
    out = nc.dram_tensor("out_0", arrays["in_x"].shape, F32, kind="ExternalOutput").ap()
    program(nc, aps, out)
    r = run(nc, [arrays], core_ids=[0])
    return r.results[0]["out_0"]
```
